# Optimizing a Trainium2 kernel written in Bass

```python
import numpy as np
import jax
import jax.numpy as jnp

def _softmax(x, axis=-1):
    return jax.nn.softmax(x, axis=axis)

def _gelu(x):
    return jax.nn.gelu(x, approximate=True)

def _silu(x):
    return jax.nn.silu(x)

def _sigmoid(x):
    return jax.nn.sigmoid(x)

def _layernorm(x, axis=-1, eps=1e-05):
    m = jnp.mean(x, axis=axis, keepdims=True)
    v = jnp.var(x, axis=axis, keepdims=True)
    return (x - m) / jnp.sqrt(v + eps)

def _scatter_add(tgt, idx, src, axis=0):
    return tgt.at[idx].add(src)

def _segment_sum(src, seg, n):
    return jax.ops.segment_sum(src, seg, n)
kernel_name = 'mk_seq_postln_d1_jaxref_r8_5413f3'

def setup_inputs(seed: int=0):
    np.random.seed(seed)
    _w = jnp.asarray

    def _L0_attn_setup():
        import jax, jax.numpy as jnp
        import numpy as np
        DIM = 256
        HEADS = 16
        DIM_HEAD = 128
        INNER = HEADS * DIM_HEAD

        def rotate_half(x):
            x1, x2 = jnp.split(x, 2, axis=-1)
            return jnp.concatenate((-x2, x1), axis=-1)

        def rotary_pos(n, dim_head, dtype):
            inv_freq = 1.0 / 10000.0 ** (jnp.arange(0, dim_head, 2, dtype=jnp.float32) / dim_head)
            seq = jnp.arange(n, dtype=jnp.float32)
            freqs = jnp.einsum('i,j->ij', seq, inv_freq)
            return jnp.concatenate((freqs, freqs), axis=-1).astype(dtype)

        def apply_rotary(pos, t):
            return t * jnp.cos(pos) + rotate_half(t) * jnp.sin(pos)
        key = jax.random.key(seed)
        ks = jax.random.split(key, 9)
        s = 0.02
        return {'x': jax.random.normal(ks[0], (2, 256, DIM), dtype=jnp.float32), 'Wq': jax.random.normal(ks[1], (DIM, INNER), dtype=jnp.float32) * s, 'bq': jnp.zeros((INNER,), dtype=jnp.float32), 'Wk': jax.random.normal(ks[2], (DIM, INNER), dtype=jnp.float32) * s, 'bk': jnp.zeros((INNER,), dtype=jnp.float32), 'Wv': jax.random.normal(ks[3], (DIM, INNER), dtype=jnp.float32) * s, 'bv': jnp.zeros((INNER,), dtype=jnp.float32), 'Wo': jax.random.normal(ks[4], (INNER, DIM), dtype=jnp.float32) * s, 'bo': jnp.zeros((DIM,), dtype=jnp.float32)}
    _L0_attn_in = _L0_attn_setup()

    def _L0_ffn_setup():
        import jax, jax.numpy as jnp
        import numpy as np
        HIDDEN = 256
        INTER = 1024
        B, S = (4, 128)

        def _qmatmul(x, w_int8, scale):
            y = jnp.einsum('bsh,ho->bso', x, w_int8.astype(x.dtype))
            return y * scale
        key = jax.random.key(seed)
        ks = jax.random.split(key, 7)
        x = jax.random.normal(ks[0], (B, S, HIDDEN), dtype=jnp.float32)
        w_gate = jax.random.randint(ks[1], (HIDDEN, INTER), -128, 128, dtype=jnp.int32).astype(jnp.int8)
        w_up = jax.random.randint(ks[2], (HIDDEN, INTER), -128, 128, dtype=jnp.int32).astype(jnp.int8)
        w_down = jax.random.randint(ks[3], (INTER, HIDDEN), -128, 128, dtype=jnp.int32).astype(jnp.int8)
        s_gate = jax.random.uniform(ks[4], (INTER,), dtype=jnp.float32) * 0.02 + 0.001
        s_up = jax.random.uniform(ks[5], (INTER,), dtype=jnp.float32) * 0.02 + 0.001
        s_down = jax.random.uniform(ks[6], (HIDDEN,), dtype=jnp.float32) * 0.02 + 0.001
        return {'x': x, 'w_gate': w_gate, 'w_up': w_up, 'w_down': w_down, 's_gate': s_gate, 's_up': s_up, 's_down': s_down}
    _L0_ffn_in = _L0_ffn_setup()
    _d = {'L0_attn_x': _L0_attn_in['x'], 'L0_attn_Wq': _L0_attn_in['Wq'], 'L0_attn_bq': _L0_attn_in['bq'], 'L0_attn_Wk': _L0_attn_in['Wk'], 'L0_attn_bk': _L0_attn_in['bk'], 'L0_attn_Wv': _L0_attn_in['Wv'], 'L0_attn_bv': _L0_attn_in['bv'], 'L0_attn_Wo': _L0_attn_in['Wo'], 'L0_attn_bo': _L0_attn_in['bo'], 'L0_ffn_w_gate': _L0_ffn_in['w_gate'], 'L0_ffn_w_up': _L0_ffn_in['w_up'], 'L0_ffn_w_down': _L0_ffn_in['w_down'], 'L0_ffn_s_gate': _L0_ffn_in['s_gate'], 'L0_ffn_s_up': _L0_ffn_in['s_up'], 'L0_ffn_s_down': _L0_ffn_in['s_down']}
    _x0 = _d['L0_attn_x']
    _d['L0_attn_x'] = jax.random.normal(jax.random.fold_in(jax.random.key(seed), 1), (4, 1024, 256), dtype=_x0.dtype)
    del _x0
    return _d

def reference(L0_attn_x, L0_attn_Wq, L0_attn_bq, L0_attn_Wk, L0_attn_bk, L0_attn_Wv, L0_attn_bv, L0_attn_Wo, L0_attn_bo, L0_ffn_w_gate, L0_ffn_w_up, L0_ffn_w_down, L0_ffn_s_gate, L0_ffn_s_up, L0_ffn_s_down):

    def _L0_attn_ref(x, Wq, bq, Wk, bk, Wv, bv, Wo, bo):
        import jax, jax.numpy as jnp
        import numpy as np
        DIM = 256
        HEADS = 16
        DIM_HEAD = 128
        INNER = HEADS * DIM_HEAD

        def rotate_half(x):
            x1, x2 = jnp.split(x, 2, axis=-1)
            return jnp.concatenate((-x2, x1), axis=-1)

        def rotary_pos(n, dim_head, dtype):
            inv_freq = 1.0 / 10000.0 ** (jnp.arange(0, dim_head, 2, dtype=jnp.float32) / dim_head)
            seq = jnp.arange(n, dtype=jnp.float32)
            freqs = jnp.einsum('i,j->ij', seq, inv_freq)
            return jnp.concatenate((freqs, freqs), axis=-1).astype(dtype)

        def apply_rotary(pos, t):
            return t * jnp.cos(pos) + rotate_half(t) * jnp.sin(pos)
        b, n, _ = x.shape
        scale = DIM_HEAD ** (-0.5)

        def proj(W, bias):
            t = x @ W + bias
            return t.reshape(b, n, HEADS, DIM_HEAD).transpose(0, 2, 1, 3)
        q = proj(Wq, bq) * scale
        k = proj(Wk, bk)
        v = proj(Wv, bv)
        pos = rotary_pos(n, DIM_HEAD, x.dtype)
        q = apply_rotary(pos, q)
        k = apply_rotary(pos, k)
        sim = jnp.einsum('bhid,bhjd->bhij', q, k)
        causal = jnp.triu(jnp.ones((n, n), dtype=bool), k=1)
        sim = jnp.where(causal, -jnp.finfo(sim.dtype).max, sim)
        attn = jax.nn.softmax(sim, axis=-1)
        out = jnp.einsum('bhij,bhjd->bhid', attn, v)
        out = out.transpose(0, 2, 1, 3).reshape(b, n, INNER)
        return out @ Wo + bo

    def _L0_ffn_ref(x, w_gate, w_up, w_down, s_gate, s_up, s_down):
        import jax, jax.numpy as jnp
        import numpy as np
        HIDDEN = 256
        INTER = 1024
        B, S = (4, 128)

        def _qmatmul(x, w_int8, scale):
            y = jnp.einsum('bsh,ho->bso', x, w_int8.astype(x.dtype))
            return y * scale
        gate = jax.nn.silu(_qmatmul(x, w_gate, s_gate))
        up = _qmatmul(x, w_up, s_up)
        fuse = gate * up
        return _qmatmul(fuse, w_down, s_down)
    x = L0_attn_x
    x = _layernorm(x + _L0_attn_ref(x, L0_attn_Wq, L0_attn_bq, L0_attn_Wk, L0_attn_bk, L0_attn_Wv, L0_attn_bv, L0_attn_Wo, L0_attn_bo), axis=-1)
    x = _layernorm(x + _L0_ffn_ref(x, L0_ffn_w_gate, L0_ffn_w_up, L0_ffn_w_down, L0_ffn_s_gate, L0_ffn_s_up, L0_ffn_s_down), axis=-1)
    return x

_drawn_inputs = setup_inputs


def setup_inputs(seed=0):
    import zlib

    import numpy as np

    out = dict(_drawn_inputs(seed))
    spreads = {'L0_attn_bq': (0.0, 0.8),
     'L0_attn_bk': (0.0, 0.8),
     'L0_attn_bv': (0.0, 0.1),
     'L0_attn_bo': (0.0, 0.1)}
    factors = {'L0_attn_Wq': 8.0, 'L0_attn_Wk': 8.0}
    for name, (base, spread) in spreads.items():
        noise = np.random.default_rng([zlib.crc32(name.encode()), seed]).standard_normal(out[name].shape)
        drawn = base * np.exp(spread * noise) if base else spread * noise
        out[name] = jnp.asarray(drawn.astype(out[name].dtype))
    for name, factor in factors.items():
        out[name] = (out[name] * factor).astype(out[name].dtype)
    return out
```

```python
import numpy as np
import concourse.bass as bass
from concourse import mybir

F32, F32R, BF16, I8 = mybir.dt.float32, mybir.dt.float32r, mybir.dt.bfloat16, mybir.dt.int8
ACT, ALU, AX = mybir.ActivationFunctionType, mybir.AluOpType, mybir.AxisListType

B, N, DIM = 4, 1024, 256
H, D = 16, 128
P = 128
KT = DIM // P
NT = N // P
GQ = 512
TPG = GQ // P
HEADS = B * H
PAIRS = HEADS // 2
INTER = 1024
JT = INTER // P
FG = B * N // GQ
SCALE = D ** -0.5
EPS = 1e-5
MASKED = -1e38
WQKV = 3 * KT * P


def layer(nc, x_rows, x_cols, w_heads, bias_qk, bias_v, wo_heads, bias_o, wg8, wu8, wd8, s_gate, s_up,
          s_down, rope_cos, rope_sin, ident_in, mask_in, out):
    def sb(name, shape, dt=F32):
        return nc.alloc_sbuf_tensor(name, shape, dt)

    def pb(name, cols):
        return nc.alloc_psum_tensor(name, [P, cols], F32)

    def sem(name):
        return nc.alloc_semaphore(name)

    w_split = nc.dram_tensor("w_split", (H, P, 2 * WQKV), F32).ap()
    wo_split = nc.dram_tensor("wo_split", (H // 2, P, 4 * DIM), F32).ap()
    x_split = nc.dram_tensor("x_split", (B, P, 2 * KT * N), F32).ap()
    recip_d = nc.dram_tensor("recip_d", (2, GQ), F32).ap()

    xT = [sb(f"xT{s}", [P, 2, KT, N], F32R) for s in "AB"]
    W = [sb(f"W{s}", [P, 3, 2, KT, P], F32R) for s in "AB"]
    WO = sb("WO", [P, 2, 2, DIM], F32R)
    QK = [sb(f"QK{s}", [P, 2, 2, N], F32R) for s in "AB"]
    V = [sb(f"V{s}", [P, 2, NT, P], F32R) for s in "AB"]
    OT = [sb(f"OT{s}", [P, 2, N], F32R) for s in "AB"]
    prob_at = [[P * sum(TPG * g + z + 1 for z in range(i)) for i in range(TPG + 1)] for g in range(2)]
    prob = [sb(f"prob{g}", [P, prob_at[g][TPG]]) for g in range(2)]
    PT = sb("PT", [P, 2, 2, GQ], F32R)
    resid = sb("resid", [P, B * NT, DIM])
    cos_t = sb("cos_t", [P, N])
    sin_t = sb("sin_t", [P, N])
    proj = sb("proj", [P, 2, GQ])
    swap = sb("swap", [P, 2, GQ])
    rot = sb("rot", [P, 4, GQ])
    norm_o = sb("norm_o", [P, 2, GQ])
    recip_b = sb("recip_b", [P, 2, GQ])
    ident = sb("ident", [P, P])
    ident_b = sb("ident_b", [P, P], BF16)
    mask_b = sb("mask_b", [P, P], BF16)
    bqk = sb("bqk", [P, 2, H])
    bias_m = sb("bias_m", [P, 2, 2])
    bv_t = sb("bv_t", [P, H])
    neg_max = sb("neg_max", [P, NT])
    row_sum = sb("row_sum", [P, NT])
    recip = sb("recip", [P, 2, TPG])
    w8, w32 = (prob[1][:, 0:3 * KT * INTER // 4].bitcast(t).rearrange("p (w n) -> p w n", w=3)
               for t in (I8, mybir.dt.int32))
    sg_t = sb("sg_t", [P, 2, JT])
    bo_b = sb("bo_b", [P, DIM])
    sd_b = sb("sd_b", [P, DIM])
    stats = sb("stats", [P, 6])
    mv = sb("mv", [P, 2, TPG, 2])
    var_eps = sb("var_eps", [P, 2, TPG])
    rstd = sb("rstd", [P, 2, TPG])
    minus_half = sb("minus_half", [P, TPG])

    S = [pb("S0", N), pb("S1", N)]
    TP = [pb("TP0", GQ), pb("TP1", GQ)]
    O = pb("O", GQ)
    PJ = pb("PJ", GQ)

    consts_in, split_out, resid_in = (sem(n) for n in ("consts_in", "split_out", "resid_in"))
    raw_in = [sem("raw_in0"), sem("raw_in1")]
    pro_hi, pro_lo, bv_used, pro_m = (sem(n) for n in ("pro_hi", "pro_lo", "bv_used", "pro_m"))
    W_in = [sem("WA_in"), sem("WB_in")]
    xT_in = [sem("xTA_in"), sem("xTB_in")]
    WO_in = sem("WO_in")
    scored, transposed, attended, chunked, v_made, wo_made = (
        sem(n) for n in ("scored", "transposed", "attended", "chunked", "v_made", "wo_made"))
    exped, pt_hi, chunk_sb, rot_hi, v_hi, o_hi = (
        sem(n) for n in ("exped", "pt_hi", "chunk_sb", "rot_hi", "v_hi", "o_hi"))
    maxed, pt_lo, cos_done, rot_done, v_lo, o_norm, recip_ok, added = (
        sem(n) for n in ("maxed", "pt_lo", "cos_done", "rot_done", "v_lo", "o_norm", "recip_ok", "added"))
    bias_at = sem("bias_at")
    sin_done, rot_lo, o_lo = (sem(n) for n in ("sin_done", "rot_lo", "o_lo"))
    swapped = [sem("swapped0"), sem("swapped1")]
    recip_out = sem("recip_out")
    recip_in = [sem("recip_in0"), sem("recip_in1")]

    def n_scored(n, s):
        return 8 * n + (s + 1)

    def n_step(n, k):
        return 12 * n + (k + 1 - 8)

    def n_four(m, c):
        return 4 * m + (c + 1)

    def n_group(n, g):
        return 2 * n + (g + 1)

    def n_added(n, i):
        return 4 * (n - 2) + (8 + i + 1)

    def wait(e, s, value):
        if not (isinstance(value, int) and value <= 0):
            e.wait_ge(s, value)

    def timelines(e, run):
        run(-1, 1, False, False, True, False)
        run(0, 0, True, False, True, False)
        run(1, 1, True, True, True, False)
        with e.Fori(1, PAIRS - 1) as it:
            run(it * 2, 0, True, True, True, True)
            run(it * 2 + 1, 1, True, True, True, False)
        run(HEADS - 2, 0, True, True, True, True)
        run(HEADS - 1, 1, True, True, False, False)
        run(HEADS, 0, False, True, False, True)

    WO_TILES = {1: [0], 2: [1], 3: [2], 4: [3], 5: [4], 6: [5], 7: [6, 7]}
    def step(k):
        g, j = (1, k) if k < 8 else (0, k - 8)
        return g, j, max(0, j - TPG * g) * P

    pieces = [("x", (b, t)) for b in range(B) for t in range(KT)] + [("w", h) for h in range(H)] \
        + [("wo", q) for q in range(H // 2)]
    raw_cols = {"x": N, "w": WQKV, "wo": 2 * DIM}

    rawW, rawX = prob[1], prob[0]
    splitW = QK[0].ap().rearrange("p a b n -> p (a b n)")
    splitX = QK[1].ap().rearrange("p a b n -> p (a b n)")

    def raw_buf(i):
        return (rawW, rawX)[i % 2][:, 0:raw_cols[pieces[i][0]]]

    def split_views(i):
        kind, cols = pieces[i][0], raw_cols[pieces[i][0]]
        groups = {"x": 1, "w": 3, "wo": 2}[kind]
        parts = (splitW, splitX)[i % 2][:, 0:2 * cols].rearrange("p (q a n) -> p q a n", q=groups, a=2)
        return parts[:, :, 0, :], parts[:, :, 1, :], raw_buf(i).rearrange("p (q n) -> p q n", q=groups)

    flat_x = [x[:, a, :, :].rearrange("p t n -> p (t n)") for x in xT for a in range(2)]
    ffn_w = flat_x[0:3]
    x1T = flat_x[3].rearrange("p (a t q) -> p a t q", a=2, t=KT)
    fuse = [q[:, :, :, :].rearrange("p a b n -> p (a b n)").rearrange("p (a j q) -> p a j q", a=2, q=GQ)
            for q in QK]
    fuse_f, silu, down_s = proj, swap, norm_o[:, 0, 0:DIM]
    x1 = rot[:, :, 0:DIM]
    x1_in, powed, half_in = sem("x1_in"), sem("powed"), sem("half_in")
    w8_in = sem("w8_in")
    LN1, LN2 = 3 * TPG + 1, 4 * TPG + 1
    w_ready, ln, x1_done, y_done, out_done = (sem(n) for n in ("w_ready", "ln", "x1_done", "y_done", "out_done"))
    xt_up, xt_hi, xt_lo, gate_up, silued, fused, fuse_hi, fuse_lo, downed = (
        sem(n) for n in ("xt_up", "xt_hi", "xt_lo", "gate_up", "silued", "fused", "fuse_hi", "fuse_lo", "downed"))

    with nc.Block() as block:

        @block.sync
        def _(sp):
            for dst, src in ((ident[:, :], ident_in), (cos_t[:, :], rope_cos), (sin_t[:, :], rope_sin),
                             (bqk[:, :, :], bias_qk), (bv_t[:, :], bias_v), (sg_t[:, 0, :], s_gate),
                             (sg_t[:, 1, :], s_up), (rot[:, 0, 0:P], mask_in),
                             (bo_b[:, :], bias_o.to_broadcast([P, DIM])),
                             (sd_b[:, :], s_down.to_broadcast([P, DIM]))):
                sp.dma_start(dst, src).then_inc(consts_in, 16)
            for b in range(B):
                sp.dma_start(resid[:, b * NT:(b + 1) * NT, :], x_rows[b]).then_inc(resid_in, 16)

            for i, (kind, idx) in enumerate(pieces):
                src = (splitW, splitX)[i % 2][:, 0:2 * raw_cols[kind]].bitcast(F32)
                wait(sp, pro_lo, i + 1)
                if kind == "x":
                    b, t = idx
                    dst = x_split[b].rearrange("p (a t n) -> p a t n", a=2, t=KT)[:, :, t, :]
                    src = src.rearrange("p (a n) -> p a n", a=2)
                else:
                    dst = (w_split if kind == "w" else wo_split)[idx]
                sp.dma_start(dst, src).then_inc(split_out, 16)
                wait(sp, split_out, 16 * (i + 1))
            sp.dma_start(xT[1][:, :, :, :].bitcast(F32).rearrange("p a t n -> p (a t n)"),
                         x_split[0]).then_inc(xT_in[1], 16)
            sp.dma_start(xT[0][:, :, :, :].bitcast(F32).rearrange("p a t n -> p (a t n)"),
                         x_split[0]).then_inc(xT_in[0], 16)

            def run(n, par, own, prev, project, out_proj, next_x=None):
                for s in range(8):
                    if project and s < 4:
                        m, c = n + 1, s
                        wait(sp, chunk_sb, n_four(m, c))
                        for lo, hi in ((0, D // 2), (D // 2, 0)):
                            sp.dma_start(swap[lo:lo + D // 2, c % 2, :],
                                         proj[hi:hi + D // 2, c % 2, :]).then_inc(swapped[c % 2], 16)
                    if prev and s in (1, 2):
                        reciprocals(n - 1, 1, s == 1)
                    if own and s in (4, 5):
                        reciprocals(n, 0, s == 4)
                    if s == 0 and next_x is not None:
                        b, x = next_x
                        wait(sp, v_made, n_four(n, 3))
                        sp.dma_start(x[:, :, :, :].bitcast(F32).rearrange("p a t n -> p (a t n)"),
                                     x_split[bass.ds(b, 1), :, :].rearrange("b p n -> (b p) n")
                                     ).then_inc(xT_in[1 if par == 0 else 0], 16)

            def reciprocals(n, g, out_part):
                if out_part:
                    wait(sp, recip_ok, n_group(n, g))
                    sp.dma_start(recip_d[g].rearrange("(p t) -> p t", p=P), recip[:, g, :]
                                 ).then_inc(recip_out, 16)
                else:
                    wait(sp, recip_out, 16 * n_group(n, g))
                    sp.dma_start(recip_b[:, g, :], recip_d[g:g + 1, :].to_broadcast([P, GQ])
                                 ).then_inc(recip_in[g], 16)

            run(-1, 1, False, False, True, False)
            run(0, 0, True, False, True, False)
            run(1, 1, True, True, True, False)
            with sp.Fori(1, H // 2 - 1) as it:
                run(it * 2, 0, True, True, True, True)
                run(it * 2 + 1, 1, True, True, True, False)
            with sp.Fori(0, B - 1) as b:
                last = b * H + (H - 2)
                run(last, 0, True, True, True, True, next_x=(b + 1, xT[1]))
                run(last + 1, 1, True, True, True, False, next_x=(b + 1, xT[0]))
                with sp.Fori(1, H // 2) as it:
                    first = b * H + it * 2 + (H - 2)
                    run(first, 0, True, True, True, True)
                    run(first + 1, 1, True, True, True, False)
            run(HEADS - 2, 0, True, True, True, True)
            run(HEADS - 1, 1, True, True, False, False)
            run(HEADS, 0, False, True, False, True)

            sp.wait_ge(transposed, n_step(HEADS, 7))
            for i, src in enumerate((wg8, wu8, wd8)):
                sp.dma_start(w32[:, i, :], src).then_inc(w8_in, 16)
            out_v = out.rearrange("(g t p) c -> g p t c", t=TPG, p=P)
            with sp.Fori(0, FG) as g:
                sp.wait_ge(y_done, 4 * g + 4)
                sp.dma_start(out_v[bass.ds(g, 1)].rearrange("g p t c -> (g p) t c"),
                             resid[:, bass.ds(g * TPG, TPG), :]).then_inc(out_done, 16)
            sp.wait_ge(out_done, 16 * FG)

        @block.gpsimd
        def _(pool):
            def run(n, par, own, prev, project, out_proj):
                m = n + 1
                for s in range(8):
                    if prev and s in (1, 5):
                        g = s // 4
                        q, o = (1 - par) , slice(g * GQ, (g + 1) * GQ)
                        wait(pool, o_hi, n_group(n - 1, g))
                        nc.gpsimd.tensor_tensor(OT[q][:, 1, o], norm_o[:, g, :], OT[q][:, 0, o].bitcast(F32),
                                                ALU.subtract).then_inc(o_lo, 1)
                    if project and 1 <= s < 5:
                        c = s - 1
                        wait(pool, swapped[c % 2], 32 * (2 * m + (c // 2 + 1)))
                        half = slice((c // 2) * GQ, (c // 2 + 1) * GQ)
                        nc.gpsimd.tensor_tensor(swap[:, c % 2, :], swap[:, c % 2, :], sin_t[:, half],
                                                ALU.mult).then_inc(sin_done, 1)
                    if project and 3 <= s < 7:
                        c = s - 3
                        wait(pool, rot_hi, n_four(m, c))
                        half = slice((c // 2) * GQ, (c // 2 + 1) * GQ)
                        q = QK[1 - par]
                        nc.gpsimd.tensor_tensor(q[:, c % 2, 1, half], rot[:, c, :],
                                                q[:, c % 2, 0, half].bitcast(F32),
                                                ALU.subtract).then_inc(rot_lo, 1)

            wait(pool, consts_in, 16 * 10)
            timelines(pool, run)
            nc.gpsimd.memset(minus_half[:, :], -0.5).then_inc(half_in, 1)
            pool.wait_ge(half_in, 1)

            def inverse_root(which, chain):
                wait(pool, ln, chain)
                nc.gpsimd.tensor_tensor(rstd[:, which, :], var_eps[:, which, :], minus_half[:, :],
                                        ALU.pow).then_inc(powed, 1)

            inverse_root(0, LN1)

            def gates(g, more):
                for j in range(JT):
                    wait(pool, fuse_hi, 8 * g + (j + 1))
                    nc.gpsimd.tensor_tensor(fuse[j % 2][:, 1, j // 2, :], fuse_f[:, j % 2, :],
                                            fuse[j % 2][:, 0, j // 2, :].bitcast(F32),
                                            ALU.subtract).then_inc(fuse_lo, 1)
                    if more and j == 3:
                        inverse_root(0, g * (LN1 + LN2) + 2 * LN1)
                inverse_root(1, g * (LN1 + LN2) + ((2 if more else 1) * LN1 + LN2))

            gates(0, True)
            with pool.Fori(1, FG - 1) as g:
                gates(g, True)
            gates(FG - 1, False)

        @block.scalar
        def _(act):
            copy = lambda o, i: nc.scalar.activation(o, i, ACT.Copy)
            for i in range(len(pieces) + 1):
                if i < len(pieces):
                    kind, idx = pieces[i]
                    wait(act, pro_lo, i - 1)
                    if kind == "wo":
                        wait(act, bv_used, idx - 1)
                    src = {"w": w_heads, "wo": wo_heads}[kind][idx] if kind != "x" else x_cols[idx[0], idx[1]]
                    act.dma_start(raw_buf(i), src).then_inc(raw_in[i % 2], 16)
                if i >= 1:
                    wait(act, raw_in[(i - 1) % 2], 16 * ((i - 1) // 2 + 1))
                    wait(act, split_out, 16 * (i - 2))
                    hi, lo, raw = split_views(i - 1)
                    copy(hi, raw).then_inc(pro_hi, 1)
            act.wait_ge(bv_used, H // 2)
            act.wait_ge(split_out, 16 * len(pieces))
            act.dma_start(W[0][:, :, :, :, :].bitcast(F32).rearrange("p q a t c -> p (q a t c)"),
                          w_split[0]).then_inc(W_in[0], 16)
            wait(act, pro_m, 2)

            def run(n, par, own, prev, project, out_proj):
                m, nxt = n + 1, 1 - par
                if project:
                    at = slice(m % H, m % H + 1) if isinstance(m, int) else bass.ds(m & (H - 1), 1)
                    nc.scalar.copy(bias_m[:, nxt, :], bqk[:, :, at].rearrange("p b h -> p (b h)")
                                   ).then_inc(bias_at, 1)
                    wait(act, bias_at, m + 1)
                for s in range(8):
                    if s < 4:
                        if prev and s > 0:
                            probs_hi(n, 2 * s)
                        if own:
                            softmax(n, s)
                        if project:
                            chunk_out(m, nxt, s)
                        if prev and s == 0:
                            probs_hi(n, 0)
                        if prev:
                            probs_hi(n, 2 * s + 1)
                    else:
                        if project:
                            v = s - 4
                            wait(act, v_made, n_four(m, v))
                            wait(act, attended, n_step(n, 7))
                            copy(V[nxt][:, 0, 2 * v:2 * v + 2, :].rearrange("p t d -> p (t d)"),
                                 PJ[:, 0:2 * P]).then_inc(v_hi, 1)
                        if own:
                            probs_hi(n, s + 4)
                    if project and 3 <= s < 7:
                        c = s - 3
                        half = slice((c // 2) * GQ, (c // 2 + 1) * GQ)
                        wait(act, rot_done, n_four(m, c))
                        copy(QK[nxt][:, c % 2, 0, half], rot[:, c, :]).then_inc(rot_hi, 1)
                    if own and s >= 4:
                        softmax(n, s)
                    if prev and s in (0, 4):
                        g = s // 4
                        o = slice(g * GQ, (g + 1) * GQ)
                        wait(act, o_norm, n_group(n - 1, g))
                        if not isinstance(n, int) or n > 2:
                            wait(act, added, n_added(n if par == 0 else n + 1, -1))
                        copy(OT[nxt][:, 0, o], norm_o[:, g, :]).then_inc(o_hi, 1)
                    if s == 0 and n_has(n, project):
                        wait(act, v_made, n_four(n, 3))
                        wait(act, chunk_sb, n_four(n, 3))
                        act.dma_start(W[par][:, :, :, :, :].bitcast(F32).rearrange("p q a t c -> p (q a t c)"),
                                      w_split[bass.ds((n + 2) & (H - 1), 1), :, :].rearrange("b p n -> (b p) n")
                                      if not isinstance(n, int) else w_split[(n + 2) % H]
                                      ).then_inc(W_in[par], 16)
                    if s == 1 and par == 1 and own:
                        wait(act, wo_made, 4 * (n - 1))
                        pair = (n - 1) >> 1
                        act.dma_start(WO[:, :, :, :].bitcast(F32).rearrange("p h a c -> p (h a c)"),
                                      wo_split[bass.ds(pair & (H // 2 - 1), 1), :, :].rearrange("b p n -> (b p) n")
                                      if not isinstance(n, int) else wo_split[pair % (H // 2)]
                                      ).then_inc(WO_in, 16)

            def n_has(n, project):
                return project and not (isinstance(n, int) and n + 2 >= HEADS)

            def probs_hi(n, k):
                g, j, c0 = step(k)
                wait(act, transposed, n_step(n, k))
                wait(act, attended, n_step(n, k) - 2)
                copy(PT[:, k % 2, 0, c0:], TP[k % 2][:, c0:]).then_inc(pt_hi, 1)

            def softmax(n, s):
                g, i, cols = s // TPG, s % TPG, (s + 1) * P
                wait(act, maxed, n_scored(n, s))
                wait(act, transposed, n_step(n, 7) if g else n_step(n - 1, 11))
                wait(act, recip_ok, n_group(n - 1, g))
                nc.scalar.activation(prob[g][:, prob_at[g][i]:prob_at[g][i] + cols], S[s % 2][:, 0:cols], ACT.Exp,
                                     bias=neg_max[:, s:s + 1], scale=1.0,
                                     accum_out=row_sum[:, s:s + 1]).then_inc(exped, 1)

            def chunk_out(m, m_par, c):
                wait(act, chunked, n_four(m, c))
                wait(act, rot_done, n_four(m, c) - 2)
                nc.scalar.activation(proj[:, c % 2, :], S[c % 2][:, GQ:], ACT.Identity,
                                     bias=bias_m[:, m_par, c % 2:c % 2 + 1],
                                     scale=SCALE if c % 2 == 0 else 1.0).then_inc(chunk_sb, 1)

            timelines(act, run)

            for i, dst in enumerate(ffn_w):
                if i < 2:
                    act.wait_ge(wo_made, 8 * PAIRS)
                    act.wait_ge(w8_in, 48)
                    copy(dst, w8[:, i, :]).then_inc(w_ready, 1)
            def fixed_x1(g, t):
                at = g * TPG + t
                row = resid[:, at, :] if isinstance(at, int) else \
                    resid[:, bass.ds(at, 1), :].rearrange("p a c -> p (a c)")
                wait(act, x1_done, TPG * g + (t + 1))
                wait(act, xt_up, 2 * g)
                copy(x1[:, t, :], row).then_inc(x1_in, 1)

            for t in range(TPG):
                fixed_x1(0, t)
            act.wait_ge(xt_up, 1)
            copy(x1T[:, 0, 0, :], TP[0][:, :]).then_inc(xt_hi, 1)
            act.wait_ge(xt_up, 2)
            copy(x1T[:, 0, 1, :], TP[1][:, :]).then_inc(xt_hi, 1)

            def gates(g, more):
                for j in range(JT):
                    act.wait_ge(gate_up, 16 * g + (2 * j + 1))
                    wait(act, fused, 8 * g + (j - 1))
                    nc.scalar.activation(silu[:, j % 2, :], S[j % 2][:, 0:GQ], ACT.Silu,
                                         scale=sg_t[:, 0, j:j + 1]).then_inc(silued, 1)
                    act.wait_ge(fused, 8 * g + (j + 1))
                    wait(act, downed, 4 * g)
                    copy(fuse[j % 2][:, 0, j // 2, :], fuse_f[:, j % 2, :]).then_inc(fuse_hi, 1)
                    if more and j > TPG:
                        fixed_x1(g + 1, j - TPG - 1)
                if more:
                    fixed_x1(g + 1, 3)
                    for t in range(KT):
                        act.wait_ge(xt_up, 2 * g + (t + 3))
                        copy(x1T[:, 0, t, :], TP[t][:, :]).then_inc(xt_hi, 1)

            gates(0, True)
            with act.Fori(1, FG - 1) as g:
                gates(g, True)
            gates(FG - 1, False)

        @block.vector
        def _(dve):
            sub = lambda o, a, b: nc.vector.tensor_tensor(o, a, b, ALU.subtract)
            dve.wait_ge(consts_in, 16 * 10)
            nc.vector.tensor_copy(ident_b[:, :], ident[:, :]).then_inc(pro_m, 1)
            nc.vector.tensor_scalar(bqk[:, 0, :], bqk[:, 0, :], SCALE, None, ALU.mult).then_inc(pro_m, 1)
            nc.vector.tensor_copy(mask_b[:, :], rot[:, 0, 0:P]).then_inc(pro_m, 1)
            for i, (kind, idx) in enumerate(pieces):
                hi, lo, raw = split_views(i)
                dve.wait_ge(pro_hi, i + 1)
                sub(lo, raw, hi.bitcast(F32)).then_inc(pro_lo, 1)
            dve.wait_ge(bv_used, H // 2)
            nc.vector.tensor_tensor(bo_b[:, :], bo_b[:, :], PJ[:, 0:DIM], ALU.add).then_inc(pro_m, 1)
            dve.wait_ge(resid_in, 16 * B)
            nc.vector.memset(stats[:, :], 0.0).then_inc(added, 8)
            dve.wait_ge(pro_m, 4)

            def run(n, par, own, prev, project, out_proj):
                m, nxt = n + 1, 1 - par
                for s in range(8):
                    if s >= 4 and project:
                        v = s - 4
                        wait(dve, v_hi, n_four(m, v))
                        vs = lambda a: V[nxt][:, a, 2 * v:2 * v + 2, :].rearrange("p t d -> p (t d)")
                        sub(vs(1), PJ[:, 0:2 * P], vs(0).bitcast(F32)).then_inc(v_lo, 1)
                    if own:
                        wait(dve, scored, n_scored(n, s))
                        nc.vector.tensor_reduce(neg_max[:, s:s + 1], S[s % 2][:, 0:(s + 1) * P], AX.X, ALU.max,
                                                negate=True).then_inc(maxed, 1)
                    if prev and s in (0, 4):
                        g = s // 4
                        wait(dve, attended, n_step(n - 1, 11) if g == 0 else n_step(n, 7))
                        wait(dve, recip_in[g], 16 * n)
                        wait(dve, o_lo, n_group(n - 1, g) - 2)
                        by_tile = lambda x: x.rearrange("d (t p) -> d t p", p=P)
                        nc.vector.tensor_tensor(by_tile(norm_o[:, g, :]), by_tile(O[:, :]),
                                                recip_b[:, g, :].rearrange("d (p t) -> d t p", p=P),
                                                ALU.mult).then_inc(o_norm, 1)
                    if project and 2 <= s < 6:
                        c = s - 2
                        wait(dve, sin_done, n_four(m, c))
                        wait(dve, cos_done, n_four(m, c))
                        nc.vector.tensor_tensor(rot[:, c, :], rot[:, c, :], swap[:, c % 2, :],
                                                ALU.add).then_inc(rot_done, 1)
                    tiles = WO_TILES.get(s, []) if out_proj else []
                    if s < 4:
                        if prev:
                            probs_lo(n, 2 * s)
                        rotate_cos(s, project, m)
                        if prev:
                            probs_lo(n, 2 * s + 1)
                    else:
                        for i in tiles[:1]:
                            add_output(n, i)
                        if own:
                            probs_lo(n, s + 4)
                        rotate_cos(s, project, m)
                    if own and s == 4:
                        reciprocal(n, 0)
                    if prev and s == 1:
                        reciprocal(n - 1, 1)
                    for i in tiles[(0 if s < 4 else 1):]:
                        add_output(n, i)

            def probs_lo(n, k):
                g, j, c0 = step(k)
                wait(dve, pt_hi, n_step(n, k))
                sub(PT[:, k % 2, 1, c0:], TP[k % 2][:, c0:],
                    PT[:, k % 2, 0, c0:].bitcast(F32)).then_inc(pt_lo, 1)

            def add_output(n, i):
                wait(dve, wo_made, 4 * (n - 2) + (i + 1))
                wait(dve, added, n_added(n, -1))
                if isinstance(n, int):
                    row = resid[:, ((n - 2) // H) * NT + i, :]
                else:
                    row = resid[:, bass.ds((((n - 2) >> 4) & (B - 1)) * NT + i, 1), :].rearrange("p a c -> p (a c)")
                nc.vector.tensor_tensor(row, row, PJ[:, 0:DIM], ALU.add).then_inc(added, 1)

            def rotate_cos(s, project, m):
                if project and 1 <= s < 5:
                    c = s - 1
                    half = slice((c // 2) * GQ, (c // 2 + 1) * GQ)
                    wait(dve, chunk_sb, n_four(m, c))
                    wait(dve, rot_lo, n_four(m - 1, c))
                    nc.vector.tensor_tensor(rot[:, c, :], proj[:, c % 2, :], cos_t[:, half],
                                            ALU.mult).then_inc(cos_done, 1)

            def reciprocal(n, g):
                wait(dve, exped, n_scored(n, 4 * g + 3))
                wait(dve, recip_out, 16 * (n_group(n, g) - 2))
                nc.vector.reciprocal(recip[:, g, :], row_sum[:, 4 * g:4 * g + 4]).then_inc(recip_ok, 1)

            timelines(dve, run)

            dve.wait_ge(added, n_added(HEADS, 7))
            dve.wait_ge(w8_in, 48)
            nc.vector.tensor_copy(ffn_w[2], w8[:, 2, :]).then_inc(w_ready, 1)

            def row_of(at):
                return resid[:, at, :] if isinstance(at, int) else \
                    resid[:, bass.ds(at, 1), :].rearrange("p a c -> p (a c)")

            def moments(which, t, row, chain):
                dve.wait_ge(ln, chain)
                dve.nop(nofuse=True)
                nc.vector.bn_stats(stats[:, :], row).then_inc(ln, 1)
                dve.wait_ge(ln, chain + 1)
                dve.nop(nofuse=True)
                nc.vector.bn_aggr(mv[:, which, t, :], stats[:, :]).then_inc(ln, 1)

            def add_eps(which, chain):
                dve.wait_ge(ln, chain)
                nc.vector.tensor_scalar(var_eps[:, which, :], mv[:, which, :, 1], EPS, None,
                                        ALU.add).then_inc(ln, 1)

            def normalise(which, t, row, done):
                nc.vector.tensor_scalar(row, row, mv[:, which, t, 0:1], rstd[:, which, t:t + 1], ALU.subtract,
                                        ALU.mult).then_inc(done, 1)

            def first_sums(g, t, chain):
                row = row_of(g * TPG + t)
                wait(dve, x1_done, TPG * g)
                wait(dve, ln, chain)
                nc.vector.tensor_tensor(row, row, bo_b[:, :], ALU.add).then_inc(ln, 1)
                moments(0, t, row, chain + 1)

            for t in range(TPG):
                first_sums(0, t, 3 * t)
            add_eps(0, 3 * TPG)
            dve.wait_ge(powed, 1)
            for t in range(TPG):
                normalise(0, t, row_of(t), x1_done)
            for t in range(KT):
                dve.wait_ge(xt_hi, t + 1)
                sub(x1T[:, 1, t, :], TP[t][:, :], x1T[:, 0, t, :].bitcast(F32)).then_inc(xt_lo, 1)

            def gates(g, more):
                chain = g * (LN1 + LN2) + LN1
                for j in range(JT):
                    dve.wait_ge(gate_up, 16 * g + (2 * j + 2))
                    dve.wait_ge(silued, 8 * g + (j + 1))
                    wait(dve, fuse_lo, 8 * g + (j - 1))
                    nc.vector.scalar_tensor_tensor(fuse_f[:, j % 2, :], S[j % 2][:, GQ:], sg_t[:, 1, j:j + 1],
                                                   silu[:, j % 2, :], ALU.mult, ALU.mult).then_inc(fused, 1)
                    if more and j < TPG:
                        first_sums(g + 1, j, chain + 3 * j)
                    if more and j == TPG - 1:
                        add_eps(0, chain + 3 * TPG)
                    if more and j == TPG:
                        dve.wait_ge(powed, 2 * g + 2)
                    if more and j >= TPG:
                        normalise(0, j - TPG, row_of((g + 1) * TPG + (j - TPG)), x1_done)
                if more:
                    for t in range(KT):
                        dve.wait_ge(xt_hi, 2 * g + (t + 3))
                        sub(x1T[:, 1, t, :], TP[t][:, :], x1T[:, 0, t, :].bitcast(F32)).then_inc(xt_lo, 1)
                chain = chain + (LN1 if more else 0)
                wait(dve, y_done, TPG * g)
                for t in range(TPG):
                    row, at = row_of(g * TPG + t), chain + 4 * t
                    dve.wait_ge(downed, 4 * g + (t + 1))
                    wait(dve, ln, at)
                    nc.vector.tensor_tensor(down_s[:, :], (O, PJ)[t % 2][:, 0:DIM], sd_b[:, :],
                                            ALU.mult).then_inc(ln, 1)
                    dve.wait_ge(ln, at + 1)
                    nc.vector.tensor_tensor(row, row, down_s[:, :], ALU.add).then_inc(ln, 1)
                    moments(1, t, row, at + 2)
                add_eps(1, chain + 4 * TPG)
                dve.wait_ge(powed, 2 * g + (3 if more else 2))
                for t in range(TPG):
                    normalise(1, t, row_of(g * TPG + t), y_done)

            gates(0, True)
            with dve.Fori(1, FG - 1) as g:
                gates(g, True)
            gates(FG - 1, False)

        @block.tensor
        def _(pe):
            mm = nc.tensor.matmul
            wo_at = [i for i, (kind, _) in enumerate(pieces) if kind == "wo"]
            pe.wait_ge(consts_in, 16 * 10)
            for q, i in enumerate(wo_at):
                wait(pe, raw_in[i % 2], 16 * (i // 2 + 1))
                for h in range(2):
                    hd = 2 * q + h
                    last = mm(PJ[:, 0:DIM], bv_t[:, hd:hd + 1].to_broadcast([P, P]),
                              raw_buf(i)[:, h * DIM:(h + 1) * DIM], start=hd == 0, stop=hd == H - 1)
                last.then_inc(bv_used, 1)
            pe.wait_ge(pro_m, 3)

            def run(n, par, own, prev, project, out_proj):
                m, nxt = n + 1, 1 - par

                def scores(s):
                    q, k = QK[par][:, 0], QK[par][:, 1]
                    wait(pe, rot_lo, n_four(n, 1 if s < 4 else 3))
                    wait(pe, exped, n_scored(n, s) - 2)
                    if s >= 4:
                        wait(pe, chunk_sb, n_four(m, s % 2 + 2) if project else 0)
                    cols = (s + 1) * P
                    banks = [(a, min(a + GQ, cols)) for a in range(0, cols, GQ)]
                    for part_q, part_k in ((0, 0), (0, 1), (1, 0)):
                        for a, b in banks:
                            mm(S[s % 2][:, a:b], QK[par][:, 0, part_q, s * P:(s + 1) * P],
                               QK[par][:, 1, part_k, a:b], start=(part_q, part_k) == (0, 0),
                               stop=part_q == 1 and b != cols)
                    mm(S[s % 2][:, cols - P:cols], ident_b[:, :], mask_b[:, :], start=False, stop=True
                       ).then_inc(scored, 1)

                def transposes(k):
                    g, j, c0 = step(k)
                    wait(pe, exped, n_scored(n, 3) if g == 0 else n_scored(n - 1, 7))
                    wait(pe, pt_lo, n_step(n, k) - 2)
                    for i in range(c0 // P, TPG):
                        last = nc.tensor.transpose(TP[k % 2][:, i * P:(i + 1) * P],
                                                   prob[g][:, prob_at[g][i] + j * P:prob_at[g][i] + (j + 1) * P],
                                                   ident[:, :])
                    last.then_inc(transposed, 1)

                def attend(nn, k, who):
                    g, j, c0 = step(k)
                    if j == 0:
                        head = nn - 1 if g else nn
                        wait(pe, v_lo, n_four(head, 3))
                        wait(pe, o_norm, n_group(head, g) - 1)
                    wait(pe, pt_lo, n_step(nn, k))
                    v = V[who]
                    last_j = TPG * (g + 1) - 1
                    mm(O[:, c0:], v[:, 0, j, :], PT[:, k % 2, 0, c0:], start=j == 0, stop=False)
                    mm(O[:, c0:], v[:, 1, j, :], PT[:, k % 2, 0, c0:], start=False, stop=False)
                    mm(O[:, c0:], v[:, 0, j, :], PT[:, k % 2, 1, c0:], start=False, stop=j == last_j
                       ).then_inc(attended, 1)

                def chunk(c):
                    half = slice((c // 2) * GQ, (c // 2 + 1) * GQ)
                    if c == 0:
                        x_and_w()
                    wait(pe, exped, n_scored(n, c) - 2 if own else n_scored(n - 1, 7))
                    if c >= 2:
                        wait(pe, chunk_sb, n_four(m, c) - 2)
                    for i, (pw, px) in enumerate(((0, 0), (0, 1), (1, 0))):
                        for t in range(KT):
                            last = mm(S[c % 2][:, GQ:], W[nxt][:, c % 2, pw, t, :], xT[par][:, px, t, half],
                                      start=i == 0 and t == 0, stop=i == 2 and t == KT - 1)
                    last.then_inc(chunked, 1)

                def x_and_w():
                    it = (n + par) >> 1 if not isinstance(n, int) else (n + par) // 2
                    wait(pe, W_in[nxt], 8 * (m - nxt) + 16)
                    seq = it // 8 if isinstance(n, int) else (n + par) >> 4
                    wait(pe, xT_in[par], seq * 16 + 16)

                def v_pair(v):
                    wait(pe, v_lo, n_four(m, v) - 1)
                    wait(pe, added, pj_added(v))
                    for t2 in range(2):
                        tok = slice((2 * v + t2) * P, (2 * v + t2 + 1) * P)
                        for i, (px, pw) in enumerate(((0, 0), (0, 1), (1, 0))):
                            for t in range(KT):
                                last = mm(PJ[:, t2 * P:(t2 + 1) * P], xT[par][:, px, t, tok],
                                          W[nxt][:, 2, pw, t, :], start=i == 0 and t == 0,
                                          stop=i == 2 and t == KT - 1)
                    last.then_inc(v_made, 1)

                def pj_added(v):
                    if out_proj:
                        return n_added(n, v + 2)
                    return n_added(n + 1, -1) if par == 1 and own else 0

                def output(i, s):
                    g = i // TPG
                    if i == 0:
                        wait(pe, WO_in, 8 * (n - 2) + 16)
                    wait(pe, o_lo, n_group(n - 1, g))
                    wait(pe, added, n_added(n, i - 1))
                    wait(pe, v_lo, n_four(m, s - 4) if s >= 4 and project else n_four(n, 3) if project else
                         n_four(n - 1, 3))
                    tok = slice(i * P, (i + 1) * P)
                    order = [(h, a, b) for h in range(2) for a, b in ((0, 0), (0, 1), (1, 0))]
                    for z, (h, po, pw) in enumerate(order):
                        last = mm(PJ[:, 0:DIM], OT[h][:, po, tok], WO[:, h, pw, :], start=z == 0,
                                  stop=z == len(order) - 1)
                    last.then_inc(wo_made, 1)

                for s in range(8):
                    if s < 4:
                        if own:
                            scores(s)
                        if s == 0:
                            if prev:
                                attend(n - 1, 11, nxt)
                            if project:
                                chunk(s)
                            if prev:
                                transposes(0)
                        else:
                            if prev:
                                transposes(2 * s)
                                attend(n, 2 * s - 1, nxt)
                            if project:
                                chunk(s)
                        if prev:
                            transposes(2 * s + 1)
                            attend(n, 2 * s, nxt)
                        tiles = WO_TILES.get(s, []) if out_proj else []
                        for i in tiles:
                            output(i, s)
                    else:
                        if project:
                            v_pair(s - 4)
                        if own:
                            scores(s)
                        if s == 4 and prev:
                            attend(n, 7, nxt)
                        tiles = WO_TILES.get(s, []) if out_proj else []
                        if tiles:
                            output(tiles[0], s)
                        if own:
                            transposes(s + 4)
                        if s > 4 and own:
                            attend(n, s + 3, par)
                        for i in tiles[1:]:
                            output(i, s)

            wait(pe, pro_m, 4)
            timelines(pe, run)

            def x1_transposes(g):
                pe.wait_ge(x1_in, g * TPG + TPG)
                wait(pe, xt_lo, 2 * g)
                for t in range(KT):
                    for i in range(TPG):
                        last = nc.tensor.transpose(TP[t][:, i * P:(i + 1) * P], x1[:, i, t * P:(t + 1) * P],
                                                   ident[:, :])
                    last.then_inc(xt_up, 1)

            pe.wait_ge(added, n_added(HEADS, 7))
            x1_transposes(0)
            pe.wait_ge(w_ready, 3)

            def group(g, more):
                pe.wait_ge(xt_lo, 2 * g + 2)
                for j in range(JT):
                    wait(pe, silued, 8 * g + (j - 1))
                    wait(pe, fused, 8 * g + (j - 1))
                    for u in range(2):
                        for t in range(KT):
                            for part in range(2):
                                last = mm(S[j % 2][:, u * GQ:(u + 1) * GQ],
                                          ffn_w[u].rearrange("p (t c) -> p t c", t=KT)[:, t, j * P:(j + 1) * P],
                                          x1T[:, part, t, :], start=t == 0 and part == 0,
                                          stop=t == KT - 1 and part == 1)
                        last.then_inc(gate_up, 1)
                for i in range(TPG):
                    if more and i == 2:
                        x1_transposes(g + 1)
                    dst = (O, PJ)[i % 2]
                    wait(pe, ln, g * (LN1 + LN2) + ((2 if more else 1) * LN1 + 4 * (i - 2) + 1) if i >= 2
                         else g * (LN1 + LN2) + LN1)
                    for j in range(JT):
                        if i == 0:
                            pe.wait_ge(fuse_lo, 8 * g + (j + 1))
                        for part in range(2):
                            last = mm(dst[:, 0:DIM], fuse[j % 2][:, part, j // 2, i * P:(i + 1) * P],
                                      ffn_w[2].rearrange("p (j c) -> p j c", j=JT)[:, j, :],
                                      start=j == 0 and part == 0, stop=j == JT - 1 and part == 1)
                    last.then_inc(downed, 1)

            group(0, True)
            with pe.Fori(1, FG - 1) as g:
                group(g, True)
            group(FG - 1, False)


def rope_tables():
    inv = (1.0 / 10000.0 ** (np.arange(0, D, 2, dtype=np.float32) / np.float32(D))).astype(np.float32)
    f = (np.arange(N, dtype=np.float32)[:, None] * inv[None, :]).astype(np.float32)
    f = np.concatenate([f, f], axis=1).T.astype(np.float64)
    sign = np.where(np.arange(D) < D // 2, -1.0, 1.0)[:, None]
    return np.cos(f).astype(np.float32), (sign * np.sin(f)).astype(np.float32)


def kernel(**inputs):
    import concourse.bacc as _bacc
    from concourse.bass_utils import run_bass_kernel_spmd as _run

    a = {k.split("_", 1)[1]: np.asarray(v) for k, v in inputs.items()}
    x = a["attn_x"]
    cos, sin = rope_tables()

    def heads(w):
        return w.reshape(KT, P, H, P).transpose(2, 1, 0, 3)

    def words(w):
        return np.ascontiguousarray(w.transpose(1, 0, 2)).reshape(P, -1).view(np.int32)

    arrays = {
        "x_rows": x.reshape(B, NT, P, DIM).transpose(0, 2, 1, 3),
        "x_cols": x.transpose(0, 2, 1).reshape(B, KT, P, N),
        "w_heads": np.stack([heads(a["attn_Wq"]), heads(a["attn_Wk"]), heads(a["attn_Wv"])], axis=2
                            ).reshape(H, P, WQKV),
        "bias_qk": np.stack([a["attn_bq"].reshape(H, P).T, a["attn_bk"].reshape(H, P).T], axis=1),
        "bias_v": a["attn_bv"].reshape(H, P).T,
        "wo_heads": a["attn_Wo"].reshape(H // 2, 2, P, DIM).transpose(0, 2, 1, 3).reshape(H // 2, P, 2 * DIM),
        "bias_o": a["attn_bo"].reshape(1, DIM),
        "wg8": words(a["ffn_w_gate"].reshape(KT, P, INTER)),
        "wu8": words(a["ffn_w_up"].reshape(KT, P, INTER)),
        "wd8": words(a["ffn_w_down"].reshape(JT, P, DIM)),
        "s_gate": a["ffn_s_gate"].reshape(JT, P).T,
        "s_up": a["ffn_s_up"].reshape(JT, P).T,
        "s_down": a["ffn_s_down"].reshape(1, DIM),
        "rope_cos": cos,
        "rope_sin": sin,
        "ident_in": np.eye(P, dtype=np.float32),
        "mask_in": np.triu(np.full((P, P), MASKED, np.float32), k=1),
    }
    nc = _bacc.Bacc("TRN2", target_bir_lowering=False, num_devices=1)
    feed, args = {}, {}
    for name, v in arrays.items():
        v = np.ascontiguousarray(v)
        feed[f"in_{name}"] = v
        args[name] = nc.dram_tensor(f"in_{name}", v.shape, mybir.dt.from_np(v.dtype), kind="ExternalInput").ap()
    args["out"] = nc.dram_tensor("out", (B * N, DIM), F32, kind="ExternalOutput").ap()
    layer(nc, **args)
    r = _run(nc, [feed], core_ids=[0])
    return r.results[0]["out"].reshape(B, N, DIM)
```

```python
import numpy as np
import concourse.bass as bass
from concourse import mybir

F32, F32R, BF16, I8 = mybir.dt.float32, mybir.dt.float32r, mybir.dt.bfloat16, mybir.dt.int8
ACT, ALU, AX = mybir.ActivationFunctionType, mybir.AluOpType, mybir.AxisListType

B, N, DIM = 4, 1024, 256
H, D = 16, 128
P = 128
KT = DIM // P
NT = N // P
GQ = 512
TPG = GQ // P
HEADS = B * H
PAIRS = HEADS // 2
INTER = 1024
JT = INTER // P
FG = B * N // GQ
SCALE = D ** -0.5
EPS = 1e-5
MASKED = -1e38
WQKV = 3 * KT * P


def layer(nc, x_rows, x_cols, w_heads, bias_qk, bias_v, wo_heads, bias_o, wg8, wu8, wd8, s_gate, s_up,
          s_down, rope_cos, rope_sin, ident_in, mask_in, out):
    def sb(name, shape, dt=F32):
        return nc.alloc_sbuf_tensor(name, shape, dt)

    def pb(name, cols):
        return nc.alloc_psum_tensor(name, [P, cols], F32)

    def sem(name):
        return nc.alloc_semaphore(name)

    w_split = nc.dram_tensor("w_split", (H, P, 2 * WQKV), F32).ap()
    wo_split = nc.dram_tensor("wo_split", (H // 2, P, 4 * DIM), F32).ap()
    x_split = nc.dram_tensor("x_split", (B, P, 2 * KT * N), F32).ap()
    recip_d = nc.dram_tensor("recip_d", (2, GQ), F32).ap()

    xT = [sb(f"xT{s}", [P, 2, KT, N], F32R) for s in "AB"]
    W = [sb(f"W{s}", [P, 3, 2, KT, P], F32R) for s in "AB"]
    WO = sb("WO", [P, 2, 2, DIM], F32R)
    QK = [sb(f"QK{s}", [P, 2, 2, N], F32R) for s in "AB"]
    V = [sb(f"V{s}", [P, 2, NT, P], F32R) for s in "AB"]
    OT = [sb(f"OT{s}", [P, 2, N], F32R) for s in "AB"]
    prob_at = [[P * sum(TPG * g + z + 1 for z in range(i)) for i in range(TPG + 1)] for g in range(2)]
    prob = [sb(f"prob{g}", [P, prob_at[g][TPG]]) for g in range(2)]
    PT = sb("PT", [P, 2, 2, GQ], F32R)
    resid = sb("resid", [P, B * NT, DIM])
    cos_t = sb("cos_t", [P, N])
    sin_t = sb("sin_t", [P, N])
    proj = sb("proj", [P, 2, GQ])
    swap = sb("swap", [P, 2, GQ])
    rot = sb("rot", [P, 4, GQ])
    v_rest = sb("v_rest", [P, 2, P])
    norm_o = sb("norm_o", [P, 2, GQ])
    recip_b = sb("recip_b", [P, 2, GQ])
    ident = sb("ident", [P, P])
    ident_b = sb("ident_b", [P, P], BF16)
    mask_b = sb("mask_b", [P, P], BF16)
    bqk = sb("bqk", [P, 2, H])
    bias_m = sb("bias_m", [P, 2, 2])
    bv_t = sb("bv_t", [P, H])
    neg_max = sb("neg_max", [P, NT])
    row_sum = sb("row_sum", [P, NT])
    recip = sb("recip", [P, 2, TPG])
    w8, w32 = (prob[1][:, 0:3 * KT * INTER // 4].bitcast(t).rearrange("p (w n) -> p w n", w=3)
               for t in (I8, mybir.dt.int32))
    sg_t = sb("sg_t", [P, 2, JT])
    bo_b = sb("bo_b", [P, DIM])
    sd_b = sb("sd_b", [P, DIM])
    stats = sb("stats", [P, 6])
    mv = sb("mv", [P, 2, TPG, 2])
    var_eps = sb("var_eps", [P, 2, TPG])
    rstd = sb("rstd", [P, 2, TPG])
    minus_half = sb("minus_half", [P, TPG])

    S = [pb("S0", N), pb("S1", N)]
    TP = [pb("TP0", GQ), pb("TP1", GQ)]
    O = pb("O", GQ)
    PJ = pb("PJ", GQ)
    v_psum = PJ[:, :].rearrange("p (t a d) -> p t a d", t=2, a=2)

    consts_in, split_out, resid_in = (sem(n) for n in ("consts_in", "split_out", "resid_in"))
    raw_in = [sem("raw_in0"), sem("raw_in1")]
    pro_hi, pro_lo, bv_used, pro_m = (sem(n) for n in ("pro_hi", "pro_lo", "bv_used", "pro_m"))
    W_in = [sem("WA_in"), sem("WB_in")]
    xT_in = [sem("xTA_in"), sem("xTB_in")]
    WO_in = sem("WO_in")
    scored, transposed, attended, chunked, v_made, wo_made = (
        sem(n) for n in ("scored", "transposed", "attended", "chunked", "v_made", "wo_made"))
    exped, pt_hi, chunk_sb, rot_hi, v_hi, o_hi = (
        sem(n) for n in ("exped", "pt_hi", "chunk_sb", "rot_hi", "v_hi", "o_hi"))
    maxed, pt_lo, cos_done, rot_done, v_sub, v_lo, o_norm, recip_ok, added = (
        sem(n) for n in ("maxed", "pt_lo", "cos_done", "rot_done", "v_sub", "v_lo", "o_norm", "recip_ok", "added"))
    bias_at = sem("bias_at")
    sin_done, rot_lo, o_lo = (sem(n) for n in ("sin_done", "rot_lo", "o_lo"))
    swapped = [sem("swapped0"), sem("swapped1")]
    recip_out = sem("recip_out")
    recip_in = [sem("recip_in0"), sem("recip_in1")]

    def n_scored(n, s):
        return 8 * n + (s + 1)

    def n_step(n, k):
        return 12 * n + (k + 1 - 8)

    def n_four(m, c):
        return 4 * m + (c + 1)

    def n_group(n, g):
        return 2 * n + (g + 1)

    def n_made(n, i):
        return 2 * (n - 2) + (i + 1)

    def n_added(n, i):
        return 2 * (n - 2) + (4 + i + 1)

    def wait(e, s, value):
        if not (isinstance(value, int) and value <= 0):
            e.wait_ge(s, value)

    def timelines(e, run):
        run(-1, 1, False, False, True, False)
        run(0, 0, True, False, True, False)
        run(1, 1, True, True, True, False)
        with e.Fori(1, PAIRS - 1) as it:
            run(it * 2, 0, True, True, True, True)
            run(it * 2 + 1, 1, True, True, True, True)
        run(HEADS - 2, 0, True, True, True, True)
        run(HEADS - 1, 1, True, True, False, True)
        run(HEADS, 0, False, True, False, True)

    def output_of(n, par, s, out_proj):
        if not out_proj:
            return None
        if par == 0:
            slots = {2: 0, 3: 1, 6: 2, 7: 3} if isinstance(n, int) and n == HEADS else {2: 0, 3: 1}
        else:
            slots = {1: 2, 2: 3}
        return (n - par, slots[s]) if s in slots else None

    def output_bank(s):
        return S[(s + 1) % 2][:, GQ:]

    def step(k):
        g, j = (1, k) if k < 8 else (0, k - 8)
        return g, j, max(0, j - TPG * g) * P

    pieces = [("x", (b, t)) for b in range(B) for t in range(KT)] + [("w", h) for h in range(H)] \
        + [("wo", q) for q in range(H // 2)]
    raw_cols = {"x": N, "w": WQKV, "wo": 2 * DIM}

    rawW, rawX = prob[1], prob[0]
    splitW = QK[0].ap().rearrange("p a b n -> p (a b n)")
    splitX = QK[1].ap().rearrange("p a b n -> p (a b n)")

    def raw_buf(i):
        return (rawW, rawX)[i % 2][:, 0:raw_cols[pieces[i][0]]]

    def split_views(i):
        kind, cols = pieces[i][0], raw_cols[pieces[i][0]]
        groups = {"x": 1, "w": 3, "wo": 2}[kind]
        parts = (splitW, splitX)[i % 2][:, 0:2 * cols].rearrange("p (q a n) -> p q a n", q=groups, a=2)
        return parts[:, :, 0, :], parts[:, :, 1, :], raw_buf(i).rearrange("p (q n) -> p q n", q=groups)

    flat_x = [x[:, a, :, :].rearrange("p t n -> p (t n)") for x in xT for a in range(2)]
    ffn_w = flat_x[0:3]
    x1T = flat_x[3].rearrange("p (a t q) -> p a t q", a=2, t=KT)
    fuse = [q[:, :, :, :].rearrange("p a b n -> p (a b n)").rearrange("p (a j q) -> p a j q", a=2, q=GQ)
            for q in QK]
    fuse_f, silu, down_s = proj, swap, norm_o[:, 0, 0:DIM]
    x1 = rot[:, :, 0:DIM]
    x1_in, powed, half_in = sem("x1_in"), sem("powed"), sem("half_in")
    w8_in = sem("w8_in")
    LN1, LN2 = 3 * TPG + 1, 4 * TPG + 1
    w_ready, ln, x1_done, y_done, out_done = (sem(n) for n in ("w_ready", "ln", "x1_done", "y_done", "out_done"))
    xt_up, xt_hi, xt_lo, gate_up, silued, fused, fuse_hi, fuse_lo, downed = (
        sem(n) for n in ("xt_up", "xt_hi", "xt_lo", "gate_up", "silued", "fused", "fuse_hi", "fuse_lo", "downed"))

    with nc.Block() as block:

        @block.sync
        def _(sp):
            for dst, src in ((ident[:, :], ident_in), (cos_t[:, :], rope_cos), (sin_t[:, :], rope_sin),
                             (bqk[:, :, :], bias_qk), (bv_t[:, :], bias_v), (sg_t[:, 0, :], s_gate),
                             (sg_t[:, 1, :], s_up), (rot[:, 0, 0:P], mask_in),
                             (bo_b[:, :], bias_o.to_broadcast([P, DIM])),
                             (sd_b[:, :], s_down.to_broadcast([P, DIM]))):
                sp.dma_start(dst, src).then_inc(consts_in, 16)
            for b in range(B):
                sp.dma_start(resid[:, b * NT:(b + 1) * NT, :], x_rows[b]).then_inc(resid_in, 16)

            for i, (kind, idx) in enumerate(pieces):
                src = (splitW, splitX)[i % 2][:, 0:2 * raw_cols[kind]].bitcast(F32)
                wait(sp, pro_lo, i + 1)
                if kind == "x":
                    b, t = idx
                    dst = x_split[b].rearrange("p (a t n) -> p a t n", a=2, t=KT)[:, :, t, :]
                    src = src.rearrange("p (a n) -> p a n", a=2)
                else:
                    dst = (w_split if kind == "w" else wo_split)[idx]
                sp.dma_start(dst, src).then_inc(split_out, 16)
                wait(sp, split_out, 16 * (i + 1))
            sp.dma_start(xT[1][:, :, :, :].bitcast(F32).rearrange("p a t n -> p (a t n)"),
                         x_split[0]).then_inc(xT_in[1], 16)
            sp.dma_start(xT[0][:, :, :, :].bitcast(F32).rearrange("p a t n -> p (a t n)"),
                         x_split[0]).then_inc(xT_in[0], 16)

            def run(n, par, own, prev, project, out_proj, next_x=None):
                for s in range(8):
                    if project and s < 4:
                        m, c = n + 1, s
                        wait(sp, chunk_sb, n_four(m, c))
                        for lo, hi in ((0, D // 2), (D // 2, 0)):
                            sp.dma_start(swap[lo:lo + D // 2, c % 2, :],
                                         proj[hi:hi + D // 2, c % 2, :]).then_inc(swapped[c % 2], 16)
                    if prev and s in (1, 2):
                        reciprocals(n - 1, 1, s == 1)
                    if own and s in (4, 5):
                        reciprocals(n, 0, s == 4)
                    if s == 0 and next_x is not None:
                        b, x = next_x
                        wait(sp, v_made, n_four(n, 3))
                        sp.dma_start(x[:, :, :, :].bitcast(F32).rearrange("p a t n -> p (a t n)"),
                                     x_split[bass.ds(b, 1), :, :].rearrange("b p n -> (b p) n")
                                     ).then_inc(xT_in[1 if par == 0 else 0], 16)

            def reciprocals(n, g, out_part):
                if out_part:
                    wait(sp, recip_ok, n_group(n, g))
                    sp.dma_start(recip_d[g].rearrange("(p t) -> p t", p=P), recip[:, g, :]
                                 ).then_inc(recip_out, 16)
                else:
                    wait(sp, recip_out, 16 * n_group(n, g))
                    sp.dma_start(recip_b[:, g, :], recip_d[g:g + 1, :].to_broadcast([P, GQ])
                                 ).then_inc(recip_in[g], 16)

            run(-1, 1, False, False, True, False)
            run(0, 0, True, False, True, False)
            run(1, 1, True, True, True, False)
            with sp.Fori(1, H // 2 - 1) as it:
                run(it * 2, 0, True, True, True, True)
                run(it * 2 + 1, 1, True, True, True, False)
            with sp.Fori(0, B - 1) as b:
                last = b * H + (H - 2)
                run(last, 0, True, True, True, True, next_x=(b + 1, xT[1]))
                run(last + 1, 1, True, True, True, False, next_x=(b + 1, xT[0]))
                with sp.Fori(1, H // 2) as it:
                    first = b * H + it * 2 + (H - 2)
                    run(first, 0, True, True, True, True)
                    run(first + 1, 1, True, True, True, False)
            run(HEADS - 2, 0, True, True, True, True)
            run(HEADS - 1, 1, True, True, False, False)
            run(HEADS, 0, False, True, False, True)

            sp.wait_ge(transposed, n_step(HEADS, 7))
            for i, src in enumerate((wg8, wu8, wd8)):
                sp.dma_start(w32[:, i, :], src).then_inc(w8_in, 16)
            out_v = out.rearrange("(g t p) c -> g p t c", t=TPG, p=P)
            with sp.Fori(0, FG) as g:
                sp.wait_ge(y_done, 4 * g + 4)
                sp.dma_start(out_v[bass.ds(g, 1)].rearrange("g p t c -> (g p) t c"),
                             resid[:, bass.ds(g * TPG, TPG), :]).then_inc(out_done, 16)
            sp.wait_ge(out_done, 16 * FG)

        @block.gpsimd
        def _(pool):
            def run(n, par, own, prev, project, out_proj):
                m = n + 1
                for s in range(8):
                    if prev and s in (1, 5):
                        g = s // 4
                        q, o = (1 - par) , slice(g * GQ, (g + 1) * GQ)
                        wait(pool, o_hi, n_group(n - 1, g))
                        nc.gpsimd.tensor_tensor(OT[q][:, 1, o], norm_o[:, g, :], OT[q][:, 0, o].bitcast(F32),
                                                ALU.subtract).then_inc(o_lo, 1)
                    if project and 1 <= s < 5:
                        c = s - 1
                        wait(pool, swapped[c % 2], 32 * (2 * m + (c // 2 + 1)))
                        half = slice((c // 2) * GQ, (c // 2 + 1) * GQ)
                        nc.gpsimd.tensor_tensor(swap[:, c % 2, :], swap[:, c % 2, :], sin_t[:, half],
                                                ALU.mult).then_inc(sin_done, 1)
                    if project and 3 <= s < 7:
                        c = s - 3
                        wait(pool, rot_hi, n_four(m, c))
                        half = slice((c // 2) * GQ, (c // 2 + 1) * GQ)
                        q = QK[1 - par]
                        nc.gpsimd.tensor_tensor(q[:, c % 2, 1, half], rot[:, c, :],
                                                q[:, c % 2, 0, half].bitcast(F32),
                                                ALU.subtract).then_inc(rot_lo, 1)

            wait(pool, consts_in, 16 * 10)
            timelines(pool, run)
            nc.gpsimd.memset(minus_half[:, :], -0.5).then_inc(half_in, 1)
            pool.wait_ge(half_in, 1)

            def inverse_root(which, chain):
                wait(pool, ln, chain)
                nc.gpsimd.tensor_tensor(rstd[:, which, :], var_eps[:, which, :], minus_half[:, :],
                                        ALU.pow).then_inc(powed, 1)

            inverse_root(0, LN1)

            def gates(g, more):
                for j in range(JT):
                    wait(pool, fuse_hi, 8 * g + (j + 1))
                    nc.gpsimd.tensor_tensor(fuse[j % 2][:, 1, j // 2, :], fuse_f[:, j % 2, :],
                                            fuse[j % 2][:, 0, j // 2, :].bitcast(F32),
                                            ALU.subtract).then_inc(fuse_lo, 1)
                    if more and j == 3:
                        inverse_root(0, g * (LN1 + LN2) + 2 * LN1)
                inverse_root(1, g * (LN1 + LN2) + ((2 if more else 1) * LN1 + LN2))

            gates(0, True)
            with pool.Fori(1, FG - 1) as g:
                gates(g, True)
            gates(FG - 1, False)

        @block.scalar
        def _(act):
            copy = lambda o, i: nc.scalar.activation(o, i, ACT.Copy)
            for i in range(len(pieces) + 1):
                if i < len(pieces):
                    kind, idx = pieces[i]
                    wait(act, pro_lo, i - 1)
                    if kind == "wo":
                        wait(act, bv_used, idx - 1)
                    src = {"w": w_heads, "wo": wo_heads}[kind][idx] if kind != "x" else x_cols[idx[0], idx[1]]
                    act.dma_start(raw_buf(i), src).then_inc(raw_in[i % 2], 16)
                if i >= 1:
                    wait(act, raw_in[(i - 1) % 2], 16 * ((i - 1) // 2 + 1))
                    wait(act, split_out, 16 * (i - 2))
                    hi, lo, raw = split_views(i - 1)
                    copy(hi, raw).then_inc(pro_hi, 1)
            act.wait_ge(bv_used, H // 2)
            act.wait_ge(split_out, 16 * len(pieces))
            act.dma_start(W[0][:, :, :, :, :].bitcast(F32).rearrange("p q a t c -> p (q a t c)"),
                          w_split[0]).then_inc(W_in[0], 16)
            wait(act, pro_m, 2)

            def run(n, par, own, prev, project, out_proj):
                m, nxt = n + 1, 1 - par
                if project:
                    at = slice(m % H, m % H + 1) if isinstance(m, int) else bass.ds(m & (H - 1), 1)
                    nc.scalar.copy(bias_m[:, nxt, :], bqk[:, :, at].rearrange("p b h -> p (b h)")
                                   ).then_inc(bias_at, 1)
                    wait(act, bias_at, m + 1)
                for s in range(8):
                    if s < 4:
                        if own:
                            softmax(n, s)
                        if project:
                            chunk_out(m, nxt, s)
                        if prev:
                            probs_hi(n, 2 * s)
                            probs_hi(n, 2 * s + 1)
                    if s >= 4 and own:
                        probs_hi(n, s + 4)
                    if s >= 4 and project:
                        v = s - 4
                        wait(act, v_made, n_four(m, v))
                        wait(act, attended, n_step(n, 7))
                        copy(V[nxt][:, 0, 2 * v:2 * v + 2, :],
                             v_psum[:, :, 0, :]).then_inc(v_hi, 1)
                    if own and s >= 4:
                        softmax(n, s)
                    if prev and s in (0, 4):
                        g = s // 4
                        o = slice(g * GQ, (g + 1) * GQ)
                        wait(act, o_norm, n_group(n - 1, g))
                        if not isinstance(n, int) or n > 2:
                            wait(act, added, n_added(n, -1) if par == 0 else n_added(n - 1, 2 * g + 1))
                        copy(OT[nxt][:, 0, o], norm_o[:, g, :]).then_inc(o_hi, 1)
                    if project and 3 <= s < 7:
                        c = s - 3
                        half = slice((c // 2) * GQ, (c // 2 + 1) * GQ)
                        wait(act, rot_done, n_four(m, c))
                        copy(QK[nxt][:, c % 2, 0, half], rot[:, c, :]).then_inc(rot_hi, 1)
                    if s == 0 and n_has(n, project):
                        wait(act, v_made, n_four(n, 3))
                        wait(act, chunk_sb, n_four(n, 3))
                        act.dma_start(W[par][:, :, :, :, :].bitcast(F32).rearrange("p q a t c -> p (q a t c)"),
                                      w_split[bass.ds((n + 2) & (H - 1), 1), :, :].rearrange("b p n -> (b p) n")
                                      if not isinstance(n, int) else w_split[(n + 2) % H]
                                      ).then_inc(W_in[par], 16)
                    if s == 3 and par == 1 and own:
                        wait(act, wo_made, 2 * (n - 1))
                        pair = (n - 1) >> 1
                        act.dma_start(WO[:, :, :, :].bitcast(F32).rearrange("p h a c -> p (h a c)"),
                                      wo_split[bass.ds(pair & (H // 2 - 1), 1), :, :].rearrange("b p n -> (b p) n")
                                      if not isinstance(n, int) else wo_split[pair % (H // 2)]
                                      ).then_inc(WO_in, 16)

            def n_has(n, project):
                return project and not (isinstance(n, int) and n + 2 >= HEADS)

            def probs_hi(n, k):
                g, j, c0 = step(k)
                wait(act, transposed, n_step(n, k))
                wait(act, attended, n_step(n, k) - 2)
                copy(PT[:, k % 2, 0, c0:], TP[k % 2][:, c0:]).then_inc(pt_hi, 1)

            def softmax(n, s):
                g, i, cols = s // TPG, s % TPG, (s + 1) * P
                wait(act, maxed, n_scored(n, s))
                wait(act, transposed, n_step(n, 7) if g else n_step(n - 1, 11))
                wait(act, recip_ok, n_group(n - 1, g))
                nc.scalar.activation(prob[g][:, prob_at[g][i]:prob_at[g][i] + cols], S[s % 2][:, 0:cols], ACT.Exp,
                                     bias=neg_max[:, s:s + 1], scale=1.0,
                                     accum_out=row_sum[:, s:s + 1]).then_inc(exped, 1)

            def chunk_out(m, m_par, c):
                wait(act, chunked, n_four(m, c))
                wait(act, rot_done, n_four(m, c) - 2)
                nc.scalar.activation(proj[:, c % 2, :], S[c % 2][:, GQ:], ACT.Identity,
                                     bias=bias_m[:, m_par, c % 2:c % 2 + 1],
                                     scale=SCALE if c % 2 == 0 else 1.0).then_inc(chunk_sb, 1)

            timelines(act, run)

            for i, dst in enumerate(ffn_w):
                if i < 2:
                    act.wait_ge(wo_made, 4 * PAIRS)
                    act.wait_ge(w8_in, 48)
                    copy(dst, w8[:, i, :]).then_inc(w_ready, 1)
            def fixed_x1(g, t):
                at = g * TPG + t
                row = resid[:, at, :] if isinstance(at, int) else \
                    resid[:, bass.ds(at, 1), :].rearrange("p a c -> p (a c)")
                wait(act, x1_done, TPG * g + (t + 1))
                wait(act, xt_up, 2 * g)
                copy(x1[:, t, :], row).then_inc(x1_in, 1)

            for t in range(TPG):
                fixed_x1(0, t)
            act.wait_ge(xt_up, 1)
            copy(x1T[:, 0, 0, :], TP[0][:, :]).then_inc(xt_hi, 1)
            act.wait_ge(xt_up, 2)
            copy(x1T[:, 0, 1, :], TP[1][:, :]).then_inc(xt_hi, 1)

            def gates(g, more):
                for j in range(JT):
                    act.wait_ge(gate_up, 16 * g + (2 * j + 1))
                    wait(act, fused, 8 * g + (j - 1))
                    nc.scalar.activation(silu[:, j % 2, :], S[j % 2][:, 0:GQ], ACT.Silu,
                                         scale=sg_t[:, 0, j:j + 1]).then_inc(silued, 1)
                    act.wait_ge(fused, 8 * g + (j + 1))
                    wait(act, downed, 4 * g)
                    copy(fuse[j % 2][:, 0, j // 2, :], fuse_f[:, j % 2, :]).then_inc(fuse_hi, 1)
                    if more and j > TPG:
                        fixed_x1(g + 1, j - TPG - 1)
                if more:
                    fixed_x1(g + 1, 3)
                    for t in range(KT):
                        act.wait_ge(xt_up, 2 * g + (t + 3))
                        copy(x1T[:, 0, t, :], TP[t][:, :]).then_inc(xt_hi, 1)

            gates(0, True)
            with act.Fori(1, FG - 1) as g:
                gates(g, True)
            gates(FG - 1, False)

        @block.vector
        def _(dve):
            sub = lambda o, a, b: nc.vector.tensor_tensor(o, a, b, ALU.subtract)
            dve.wait_ge(consts_in, 16 * 10)
            nc.vector.tensor_copy(ident_b[:, :], ident[:, :]).then_inc(pro_m, 1)
            nc.vector.tensor_scalar(bqk[:, 0, :], bqk[:, 0, :], SCALE, None, ALU.mult).then_inc(pro_m, 1)
            nc.vector.tensor_copy(mask_b[:, :], rot[:, 0, 0:P]).then_inc(pro_m, 1)
            for i, (kind, idx) in enumerate(pieces):
                hi, lo, raw = split_views(i)
                dve.wait_ge(pro_hi, i + 1)
                sub(lo, raw, hi.bitcast(F32)).then_inc(pro_lo, 1)
            dve.wait_ge(bv_used, H // 2)
            nc.vector.tensor_tensor(bo_b[:, :], bo_b[:, :], PJ[:, 0:DIM], ALU.add).then_inc(pro_m, 1)
            dve.wait_ge(resid_in, 16 * B)
            nc.vector.memset(stats[:, :], 0.0).then_inc(added, 4)
            dve.wait_ge(pro_m, 4)

            def run(n, par, own, prev, project, out_proj):
                m, nxt = n + 1, 1 - par
                for s in range(8):
                    if own:
                        wait(dve, scored, n_scored(n, s))
                        nc.vector.tensor_reduce(neg_max[:, s:s + 1], S[s % 2][:, 0:(s + 1) * P], AX.X, ALU.max,
                                                negate=True).then_inc(maxed, 1)
                    if s >= 4 and own:
                        probs_lo(n, s + 4)
                    if prev and s in (0, 4):
                        g = s // 4
                        wait(dve, attended, n_step(n - 1, 11) if g == 0 else n_step(n, 7))
                        wait(dve, recip_in[g], 16 * n)
                        wait(dve, o_lo, n_group(n - 1, g) - 2)
                        by_tile = lambda x: x.rearrange("d (t p) -> d t p", p=P)
                        nc.vector.tensor_tensor(by_tile(norm_o[:, g, :]), by_tile(O[:, :]),
                                                recip_b[:, g, :].rearrange("d (p t) -> d t p", p=P),
                                                ALU.mult).then_inc(o_norm, 1)
                    if s >= 4 and project:
                        v = s - 4
                        wait(dve, v_hi, n_four(m, v))
                        wait(dve, v_lo, n_four(m, v) - 1)
                        tiles = slice(2 * v, 2 * v + 2)
                        sub(v_rest[:, :, :], v_psum[:, :, 0, :], V[nxt][:, 0, tiles, :].bitcast(F32)
                            ).then_inc(v_sub, 1)
                        wait(dve, v_sub, n_four(m, v))
                        nc.vector.tensor_tensor(V[nxt][:, 1, tiles, :], v_rest[:, :, :], v_psum[:, :, 1, :],
                                                ALU.add).then_inc(v_lo, 1)
                    if project and 2 <= s < 6:
                        c = s - 2
                        wait(dve, sin_done, n_four(m, c))
                        wait(dve, cos_done, n_four(m, c))
                        nc.vector.tensor_tensor(rot[:, c, :], rot[:, c, :], swap[:, c % 2, :],
                                                ALU.add).then_inc(rot_done, 1)
                    done = output_of(n, par, s, out_proj)
                    if done:
                        add_output(s, *done)
                    if s < 4 and prev:
                        probs_lo(n, 2 * s)
                    if s < 4 and project:
                        rotate_cos(s, m)
                    if s < 4 and prev:
                        probs_lo(n, 2 * s + 1)
                    if own and s == 4:
                        reciprocal(n, 0)
                    if prev and s == 0:
                        reciprocal(n - 1, 1)

            def probs_lo(n, k):
                g, j, c0 = step(k)
                wait(dve, pt_hi, n_step(n, k))
                sub(PT[:, k % 2, 1, c0:], TP[k % 2][:, c0:],
                    PT[:, k % 2, 0, c0:].bitcast(F32)).then_inc(pt_lo, 1)

            def add_output(s, n, i):
                wait(dve, wo_made, n_made(n, i))
                wait(dve, added, n_added(n, -1))
                if isinstance(n, int):
                    at = ((n - 2) // H) * NT + 2 * i
                    rows = resid[:, at:at + 2, :]
                else:
                    rows = resid[:, bass.ds((((n - 2) >> 4) & (B - 1)) * NT + 2 * i, 2), :]
                rows = rows.rearrange("p a c -> p (a c)")
                nc.vector.tensor_tensor(rows, rows, output_bank(s), ALU.add).then_inc(added, 1)

            def rotate_cos(c, m):
                half = slice((c // 2) * GQ, (c // 2 + 1) * GQ)
                wait(dve, chunk_sb, n_four(m, c))
                wait(dve, rot_lo, n_four(m - 1, c))
                nc.vector.tensor_tensor(rot[:, c, :], proj[:, c % 2, :], cos_t[:, half],
                                        ALU.mult).then_inc(cos_done, 1)

            def reciprocal(n, g):
                wait(dve, exped, n_scored(n, 4 * g + 3))
                wait(dve, recip_out, 16 * (n_group(n, g) - 2))
                nc.vector.reciprocal(recip[:, g, :], row_sum[:, 4 * g:4 * g + 4]).then_inc(recip_ok, 1)

            timelines(dve, run)

            dve.wait_ge(added, n_added(HEADS, 3))
            dve.wait_ge(w8_in, 48)
            nc.vector.tensor_copy(ffn_w[2], w8[:, 2, :]).then_inc(w_ready, 1)

            def row_of(at):
                return resid[:, at, :] if isinstance(at, int) else \
                    resid[:, bass.ds(at, 1), :].rearrange("p a c -> p (a c)")

            def moments(which, t, row, chain):
                dve.wait_ge(ln, chain)
                dve.nop(nofuse=True)
                nc.vector.bn_stats(stats[:, :], row).then_inc(ln, 1)
                dve.wait_ge(ln, chain + 1)
                dve.nop(nofuse=True)
                nc.vector.bn_aggr(mv[:, which, t, :], stats[:, :]).then_inc(ln, 1)

            def add_eps(which, chain):
                dve.wait_ge(ln, chain)
                nc.vector.tensor_scalar(var_eps[:, which, :], mv[:, which, :, 1], EPS, None,
                                        ALU.add).then_inc(ln, 1)

            def normalise(which, t, row, done):
                nc.vector.tensor_scalar(row, row, mv[:, which, t, 0:1], rstd[:, which, t:t + 1], ALU.subtract,
                                        ALU.mult).then_inc(done, 1)

            def first_sums(g, t, chain):
                row = row_of(g * TPG + t)
                wait(dve, x1_done, TPG * g)
                wait(dve, ln, chain)
                nc.vector.tensor_tensor(row, row, bo_b[:, :], ALU.add).then_inc(ln, 1)
                moments(0, t, row, chain + 1)

            for t in range(TPG):
                first_sums(0, t, 3 * t)
            add_eps(0, 3 * TPG)
            dve.wait_ge(powed, 1)
            for t in range(TPG):
                normalise(0, t, row_of(t), x1_done)
            for t in range(KT):
                dve.wait_ge(xt_hi, t + 1)
                sub(x1T[:, 1, t, :], TP[t][:, :], x1T[:, 0, t, :].bitcast(F32)).then_inc(xt_lo, 1)

            def gates(g, more):
                chain = g * (LN1 + LN2) + LN1
                for j in range(JT):
                    dve.wait_ge(gate_up, 16 * g + (2 * j + 2))
                    dve.wait_ge(silued, 8 * g + (j + 1))
                    wait(dve, fuse_lo, 8 * g + (j - 1))
                    nc.vector.scalar_tensor_tensor(fuse_f[:, j % 2, :], S[j % 2][:, GQ:], sg_t[:, 1, j:j + 1],
                                                   silu[:, j % 2, :], ALU.mult, ALU.mult).then_inc(fused, 1)
                    if more and j < TPG:
                        first_sums(g + 1, j, chain + 3 * j)
                    if more and j == TPG - 1:
                        add_eps(0, chain + 3 * TPG)
                    if more and j == TPG:
                        dve.wait_ge(powed, 2 * g + 2)
                    if more and j >= TPG:
                        normalise(0, j - TPG, row_of((g + 1) * TPG + (j - TPG)), x1_done)
                if more:
                    for t in range(KT):
                        dve.wait_ge(xt_hi, 2 * g + (t + 3))
                        sub(x1T[:, 1, t, :], TP[t][:, :], x1T[:, 0, t, :].bitcast(F32)).then_inc(xt_lo, 1)
                chain = chain + (LN1 if more else 0)
                wait(dve, y_done, TPG * g)
                for t in range(TPG):
                    row, at = row_of(g * TPG + t), chain + 4 * t
                    dve.wait_ge(downed, 4 * g + (t + 1))
                    wait(dve, ln, at)
                    nc.vector.tensor_tensor(down_s[:, :], (O, PJ)[t % 2][:, 0:DIM], sd_b[:, :],
                                            ALU.mult).then_inc(ln, 1)
                    dve.wait_ge(ln, at + 1)
                    nc.vector.tensor_tensor(row, row, down_s[:, :], ALU.add).then_inc(ln, 1)
                    moments(1, t, row, at + 2)
                add_eps(1, chain + 4 * TPG)
                dve.wait_ge(powed, 2 * g + (3 if more else 2))
                for t in range(TPG):
                    normalise(1, t, row_of(g * TPG + t), y_done)

            gates(0, True)
            with dve.Fori(1, FG - 1) as g:
                gates(g, True)
            gates(FG - 1, False)

        @block.tensor
        def _(pe):
            mm = nc.tensor.matmul
            wo_at = [i for i, (kind, _) in enumerate(pieces) if kind == "wo"]
            pe.wait_ge(consts_in, 16 * 10)
            for q, i in enumerate(wo_at):
                wait(pe, raw_in[i % 2], 16 * (i // 2 + 1))
                for h in range(2):
                    hd = 2 * q + h
                    last = mm(PJ[:, 0:DIM], bv_t[:, hd:hd + 1].to_broadcast([P, P]),
                              raw_buf(i)[:, h * DIM:(h + 1) * DIM], start=hd == 0, stop=hd == H - 1)
                last.then_inc(bv_used, 1)
            pe.wait_ge(pro_m, 3)

            def run(n, par, own, prev, project, out_proj):
                m, nxt = n + 1, 1 - par

                def scores(s):
                    q, k = QK[par][:, 0], QK[par][:, 1]
                    wait(pe, rot_lo, n_four(n, 1 if s < 4 else 3))
                    wait(pe, exped, n_scored(n, s) - 2)
                    if s >= 4:
                        wait(pe, chunk_sb, n_four(m, s % 2 + 2) if project else 0)
                    output_read(s)
                    cols = (s + 1) * P
                    banks = [(a, min(a + GQ, cols)) for a in range(0, cols, GQ)]
                    for part_q, part_k in ((0, 0), (0, 1), (1, 0)):
                        for a, b in banks:
                            mm(S[s % 2][:, a:b], QK[par][:, 0, part_q, s * P:(s + 1) * P],
                               QK[par][:, 1, part_k, a:b], start=(part_q, part_k) == (0, 0),
                               stop=part_q == 1 and b != cols)
                    mm(S[s % 2][:, cols - P:cols], ident_b[:, :], mask_b[:, :], start=False, stop=True
                       ).then_inc(scored, 1)

                def transposes(k):
                    g, j, c0 = step(k)
                    wait(pe, exped, n_scored(n, 3) if g == 0 else n_scored(n - 1, 7))
                    wait(pe, pt_lo, n_step(n, k) - 2)
                    for i in range(c0 // P, TPG):
                        last = nc.tensor.transpose(TP[k % 2][:, i * P:(i + 1) * P],
                                                   prob[g][:, prob_at[g][i] + j * P:prob_at[g][i] + (j + 1) * P],
                                                   ident[:, :])
                    last.then_inc(transposed, 1)

                def attend(nn, k, who):
                    g, j, c0 = step(k)
                    if j == 0:
                        head = nn - 1 if g else nn
                        wait(pe, v_lo, n_four(head, 3))
                        wait(pe, o_norm, n_group(head, g) - 1)
                    wait(pe, pt_lo, n_step(nn, k))
                    v = V[who]
                    last_j = TPG * (g + 1) - 1
                    mm(O[:, c0:], v[:, 0, j, :], PT[:, k % 2, 0, c0:], start=j == 0, stop=False)
                    mm(O[:, c0:], v[:, 1, j, :], PT[:, k % 2, 0, c0:], start=False, stop=False)
                    mm(O[:, c0:], v[:, 0, j, :], PT[:, k % 2, 1, c0:], start=False, stop=j == last_j
                       ).then_inc(attended, 1)

                def chunk(c):
                    half = slice((c // 2) * GQ, (c // 2 + 1) * GQ)
                    if c == 0:
                        x_and_w()
                    wait(pe, exped, n_scored(n, c) - 2 if own else n_scored(n - 1, 7))
                    if c >= 2:
                        wait(pe, chunk_sb, n_four(m, c) - 2)
                    output_read(c)
                    for i, (pw, px) in enumerate(((0, 0), (0, 1), (1, 0))):
                        for t in range(KT):
                            last = mm(S[c % 2][:, GQ:], W[nxt][:, c % 2, pw, t, :], xT[par][:, px, t, half],
                                      start=i == 0 and t == 0, stop=i == 2 and t == KT - 1)
                    last.then_inc(chunked, 1)

                def x_and_w():
                    it = (n + par) >> 1 if not isinstance(n, int) else (n + par) // 2
                    wait(pe, W_in[nxt], 8 * (m - nxt) + 16)
                    seq = it // 8 if isinstance(n, int) else (n + par) >> 4
                    wait(pe, xT_in[par], seq * 16 + 16)

                def v_pair(v):
                    wait(pe, v_lo, n_four(m, v) - 1)
                    for t2 in range(2):
                        tok = slice((2 * v + t2) * P, (2 * v + t2 + 1) * P)
                        w = W[nxt][:, 2]
                        mm(v_psum[:, t2, :, :], xT[par][:, 0, 0, tok], w[:, :, 0, :], start=True, stop=False)
                        for t in range(KT):
                            mm(v_psum[:, t2, 0, :], xT[par][:, 1, t, tok], w[:, 0, t, :], start=False, stop=False)
                        last = mm(v_psum[:, t2, :, :], xT[par][:, 0, 1, tok], w[:, :, 1, :],
                                  start=False, stop=True)
                    last.then_inc(v_made, 1)

                def output_read(s):
                    before = output_of(n, par, s - 1, out_proj)
                    if before:
                        wait(pe, added, n_added(*before))

                def output(s, nn, i):
                    if i == 0:
                        wait(pe, WO_in, 8 * (nn - 2) + 16)
                    wait(pe, o_lo, n_group(nn - 1, i // 2))
                    if project:
                        wait(pe, chunk_sb, n_four(m, s - 1))
                    wait(pe, added, n_added(nn, i - 1))
                    for tile in range(2):
                        tok = slice((2 * i + tile) * P, (2 * i + tile + 1) * P)
                        order = [(h, a, b) for h in range(2) for a, b in ((0, 0), (0, 1), (1, 0))]
                        for z, (h, po, pw) in enumerate(order):
                            last = mm(output_bank(s)[:, tile * DIM:(tile + 1) * DIM], OT[h][:, po, tok],
                                      WO[:, h, pw, :], start=z == 0, stop=z == len(order) - 1)
                    last.then_inc(wo_made, 1)

                for s in range(8):
                    if own:
                        scores(s)
                    if s < 4 and project:
                        chunk(s)
                    made = output_of(n, par, s, out_proj)
                    if made:
                        output(s, *made)
                    if prev and s == 0:
                        attend(n - 1, 11, nxt)
                        transposes(0)
                        transposes(1)
                    elif prev and s < 4:
                        attend(n, 2 * s - 2, nxt)
                        transposes(2 * s)
                        attend(n, 2 * s - 1, nxt)
                        transposes(2 * s + 1)
                    if s == 4 and prev:
                        attend(n, 6, nxt)
                    if s >= 4 and own:
                        transposes(s + 4)
                    if s >= 4 and project:
                        v_pair(s - 4)
                    if s == 4 and prev:
                        attend(n, 7, nxt)
                    if s > 4 and own:
                        attend(n, s + 3, par)

            wait(pe, pro_m, 4)
            timelines(pe, run)

            def x1_transposes(g):
                pe.wait_ge(x1_in, g * TPG + TPG)
                wait(pe, xt_lo, 2 * g)
                for t in range(KT):
                    for i in range(TPG):
                        last = nc.tensor.transpose(TP[t][:, i * P:(i + 1) * P], x1[:, i, t * P:(t + 1) * P],
                                                   ident[:, :])
                    last.then_inc(xt_up, 1)

            pe.wait_ge(added, n_added(HEADS, 3))
            x1_transposes(0)
            pe.wait_ge(w_ready, 3)

            def group(g, more):
                pe.wait_ge(xt_lo, 2 * g + 2)
                for j in range(JT):
                    wait(pe, silued, 8 * g + (j - 1))
                    wait(pe, fused, 8 * g + (j - 1))
                    for u in range(2):
                        for t in range(KT):
                            for part in range(2):
                                last = mm(S[j % 2][:, u * GQ:(u + 1) * GQ],
                                          ffn_w[u].rearrange("p (t c) -> p t c", t=KT)[:, t, j * P:(j + 1) * P],
                                          x1T[:, part, t, :], start=t == 0 and part == 0,
                                          stop=t == KT - 1 and part == 1)
                        last.then_inc(gate_up, 1)
                for i in range(TPG):
                    if more and i == 2:
                        x1_transposes(g + 1)
                    dst = (O, PJ)[i % 2]
                    wait(pe, ln, g * (LN1 + LN2) + ((2 if more else 1) * LN1 + 4 * (i - 2) + 1) if i >= 2
                         else g * (LN1 + LN2) + LN1)
                    for j in range(JT):
                        if i == 0:
                            pe.wait_ge(fuse_lo, 8 * g + (j + 1))
                        for part in range(2):
                            last = mm(dst[:, 0:DIM], fuse[j % 2][:, part, j // 2, i * P:(i + 1) * P],
                                      ffn_w[2].rearrange("p (j c) -> p j c", j=JT)[:, j, :],
                                      start=j == 0 and part == 0, stop=j == JT - 1 and part == 1)
                    last.then_inc(downed, 1)

            group(0, True)
            with pe.Fori(1, FG - 1) as g:
                group(g, True)
            group(FG - 1, False)


def rope_tables():
    inv = (1.0 / 10000.0 ** (np.arange(0, D, 2, dtype=np.float32) / np.float32(D))).astype(np.float32)
    f = (np.arange(N, dtype=np.float32)[:, None] * inv[None, :]).astype(np.float32)
    f = np.concatenate([f, f], axis=1).T.astype(np.float64)
    sign = np.where(np.arange(D) < D // 2, -1.0, 1.0)[:, None]
    return np.cos(f).astype(np.float32), (sign * np.sin(f)).astype(np.float32)


def kernel(**inputs):
    import concourse.bacc as _bacc
    from concourse.bass_utils import run_bass_kernel_spmd as _run

    a = {k.split("_", 1)[1]: np.asarray(v) for k, v in inputs.items()}
    x = a["attn_x"]
    cos, sin = rope_tables()

    def heads(w):
        return w.reshape(KT, P, H, P).transpose(2, 1, 0, 3)

    def words(w):
        return np.ascontiguousarray(w.transpose(1, 0, 2)).reshape(P, -1).view(np.int32)

    arrays = {
        "x_rows": x.reshape(B, NT, P, DIM).transpose(0, 2, 1, 3),
        "x_cols": x.transpose(0, 2, 1).reshape(B, KT, P, N),
        "w_heads": np.stack([heads(a["attn_Wq"]), heads(a["attn_Wk"]), heads(a["attn_Wv"])], axis=2
                            ).reshape(H, P, WQKV),
        "bias_qk": np.stack([a["attn_bq"].reshape(H, P).T, a["attn_bk"].reshape(H, P).T], axis=1),
        "bias_v": a["attn_bv"].reshape(H, P).T,
        "wo_heads": a["attn_Wo"].reshape(H // 2, 2, P, DIM).transpose(0, 2, 1, 3).reshape(H // 2, P, 2 * DIM),
        "bias_o": a["attn_bo"].reshape(1, DIM),
        "wg8": words(a["ffn_w_gate"].reshape(KT, P, INTER)),
        "wu8": words(a["ffn_w_up"].reshape(KT, P, INTER)),
        "wd8": words(a["ffn_w_down"].reshape(JT, P, DIM)),
        "s_gate": a["ffn_s_gate"].reshape(JT, P).T,
        "s_up": a["ffn_s_up"].reshape(JT, P).T,
        "s_down": a["ffn_s_down"].reshape(1, DIM),
        "rope_cos": cos,
        "rope_sin": sin,
        "ident_in": np.eye(P, dtype=np.float32),
        "mask_in": np.triu(np.full((P, P), MASKED, np.float32), k=1),
    }
    nc = _bacc.Bacc("TRN2", target_bir_lowering=False, num_devices=1)
    feed, args = {}, {}
    for name, v in arrays.items():
        v = np.ascontiguousarray(v)
        feed[f"in_{name}"] = v
        args[name] = nc.dram_tensor(f"in_{name}", v.shape, mybir.dt.from_np(v.dtype), kind="ExternalInput").ap()
    args["out"] = nc.dram_tensor("out", (B * N, DIM), F32, kind="ExternalOutput").ap()
    layer(nc, **args)
    r = _run(nc, [feed], core_ids=[0])
    return r.results[0]["out"].reshape(B, N, DIM)
```

```python
import numpy as np
import concourse.bass as bass
from concourse import mybir

F32, F32R, BF16, I8 = mybir.dt.float32, mybir.dt.float32r, mybir.dt.bfloat16, mybir.dt.int8
ACT, ALU, AX = mybir.ActivationFunctionType, mybir.AluOpType, mybir.AxisListType

B, N, DIM = 4, 1024, 256
H, D = 16, 128
P = 128
KT = DIM // P
NT = N // P
GQ = 512
TPG = GQ // P
HEADS = B * H
PAIRS = HEADS // 2
INTER = 1024
JT = INTER // P
FG = B * N // GQ
SCALE = D ** -0.5
EPS = 1e-5
MASKED = -1e38
WQKV = 3 * KT * P


def layer(nc, x_rows, x_cols, w_heads, bias_qk, bias_v, wo_heads, bias_o, wg8, wu8, wd8, s_gate, s_up,
          s_down, rope_cos, rope_sin, ident_in, mask_in, out):
    def sb(name, shape, dt=F32):
        return nc.alloc_sbuf_tensor(name, shape, dt)

    def pb(name, cols):
        return nc.alloc_psum_tensor(name, [P, cols], F32)

    def sem(name):
        return nc.alloc_semaphore(name)

    recip_d = nc.dram_tensor("recip_d", (2, GQ), F32).ap()

    xT = sb("xT", [P, 2, KT, N], F32R)
    x_raw = sb("x_raw", [P, KT, N])
    w_raw = sb("w_raw", [P, 3, KT, P])
    wo_raw = sb("wo_raw", [P, 2, DIM])
    W = [sb(f"W{s}", [P, 3, 2, KT, P], F32R) for s in "AB"]
    WO = sb("WO", [P, 2, 2, DIM], F32R)
    QK = [sb(f"QK{s}", [P, 2, 2, N], F32R) for s in "AB"]
    V = [sb(f"V{s}", [P, 2, NT, P], F32R) for s in "AB"]
    OT = [sb(f"OT{s}", [P, 2, N], F32R) for s in "AB"]
    prob_at = [[P * sum(TPG * g + z + 1 for z in range(i)) for i in range(TPG + 1)] for g in range(2)]
    prob = [sb(f"prob{g}", [P, prob_at[g][TPG]]) for g in range(2)]
    PT = sb("PT", [P, 2, 2, GQ], F32R)
    resid = sb("resid", [P, B * NT, DIM])
    cos_t = sb("cos_t", [P, N])
    sin_t = sb("sin_t", [P, N])
    proj = sb("proj", [P, 2, GQ])
    swap = sb("swap", [P, 2, GQ])
    rot = sb("rot", [P, 4, GQ])
    v_rest = sb("v_rest", [P, 2, P])
    norm_o = sb("norm_o", [P, 2, GQ])
    recip_b = sb("recip_b", [P, 2, GQ])
    ident = sb("ident", [P, P])
    ident_b = sb("ident_b", [P, P], BF16)
    mask_b = sb("mask_b", [P, P], BF16)
    zeros = sb("zeros", [P, GQ], BF16)
    bqk = sb("bqk", [P, 2, H])
    bias_m = sb("bias_m", [P, 2, 2])
    bias_o_m = sb("bias_o_m", [P, 2])
    bv_t = sb("bv_t", [P, H])
    neg_max = sb("neg_max", [P, NT])
    row_sum = sb("row_sum", [P, NT])
    recip = sb("recip", [P, 2, TPG])
    w8, w32 = (x_raw[:, :, :].rearrange("p t n -> p (t n)")[:, 0:3 * KT * INTER // 4].bitcast(t)
               .rearrange("p (w n) -> p w n", w=3) for t in (I8, mybir.dt.int32))
    sg_t = sb("sg_t", [P, 2, JT])
    bo_b = sb("bo_b", [P, DIM])
    sd_b = sb("sd_b", [P, DIM])
    stats = sb("stats", [P, 2, TPG, 6])
    mv = sb("mv", [P, 2, TPG, 2])
    var_eps = sb("var_eps", [P, 2, TPG])
    rstd = sb("rstd", [P, 2, TPG])
    minus_half = sb("minus_half", [P, TPG])

    S = [pb("S0", N), pb("S1", N)]
    TP = [pb("TP0", GQ), pb("TP1", GQ)]
    O = pb("O", GQ)
    PJ = pb("PJ", GQ)
    v_psum = PJ[:, :].rearrange("p (t a d) -> p t a d", t=2, a=2)

    consts_in, resid_in, consts_ready = (sem(n) for n in ("consts_in", "resid_in", "consts_ready"))
    W_in, x_first, x_in = sem("W_in"), sem("x_first"), sem("x_in")
    WO_in = sem("WO_in")
    w_hi, w_lo, WO_hi, WO_lo = (sem(n) for n in ("w_hi", "w_lo", "WO_hi", "WO_lo"))
    x_hi, x_lo = sem("x_hi"), sem("x_lo")
    scored, transposed, attended, chunked, v_made, wo_made = (
        sem(n) for n in ("scored", "transposed", "attended", "chunked", "v_made", "wo_made"))
    exped, pt_hi, chunk_sb, rot_hi, v_hi, o_hi = (
        sem(n) for n in ("exped", "pt_hi", "chunk_sb", "rot_hi", "v_hi", "o_hi"))
    maxed, pt_lo, cos_done, rot_done, v_sub, v_lo, o_norm, recip_ok, added = (
        sem(n) for n in ("maxed", "pt_lo", "cos_done", "rot_done", "v_sub", "v_lo", "o_norm", "recip_ok", "added"))
    bias_at, bias_o_at, o_biased = sem("bias_at"), sem("bias_o_at"), sem("o_biased")
    sin_done, rot_lo, o_lo = (sem(n) for n in ("sin_done", "rot_lo", "o_lo"))
    swapped = [sem("swapped0"), sem("swapped1")]
    recip_out = sem("recip_out")
    recip_in = [sem("recip_in0"), sem("recip_in1")]

    def n_scored(n, s):
        return 8 * n + (s + 1)

    def n_step(n, k):
        return 12 * n + (k + 1 - 8)

    def n_four(m, c):
        return 4 * m + (c + 1)

    def n_w(m, q):
        return 3 * m + (q + 1)

    def n_x(b, half):
        return b * 2 + (half + 1)

    def halves(a, part, half):
        return (a if part is None else a[:, part])[:, :, half * GQ:(half + 1) * GQ]

    def n_group(n, g):
        return 2 * n + (g + 1)

    def n_made(n, i):
        return 2 * (n - 2) + (i + 1)

    def n_added(n, i):
        return 2 * (n - 2) + (4 + i + 1)

    def wait(e, s, value):
        if not (isinstance(value, int) and value <= 0):
            e.wait_ge(s, value)

    def timelines(e, run):
        run(-1, 1, False, False, True, False)
        run(0, 0, True, False, True, False)
        run(1, 1, True, True, True, False)
        with e.Fori(1, PAIRS - 1) as it:
            run(it * 2, 0, True, True, True, True)
            run(it * 2 + 1, 1, True, True, True, True)
        run(HEADS - 2, 0, True, True, True, True)
        run(HEADS - 1, 1, True, True, False, True)
        run(HEADS, 0, False, True, False, True)

    def n_has(n, project):
        return project and not (isinstance(n, int) and n + 2 >= HEADS)

    def w_piece(n, s):
        return s - (4 if isinstance(n, int) and n < 0 else 1)

    def output_of(n, par, s, out_proj):
        if not out_proj:
            return None
        if par == 0:
            slots = {2: 0, 3: 1, 6: 2, 7: 3} if isinstance(n, int) and n == HEADS else {2: 0, 3: 1}
        else:
            slots = {1: 2, 2: 3}
        return (n - par, slots[s]) if s in slots else None

    def output_bank(s):
        return S[(s + 1) % 2][:, GQ:]

    def step(k):
        g, j = (1, k) if k < 8 else (0, k - 8)
        return g, j, max(0, j - TPG * g) * P

    def sequence_timelines(e, run):
        run(-1, 1, False, False, True, False)
        run(0, 0, True, False, True, False)
        run(1, 1, True, True, True, False)
        with e.Fori(1, H // 2 - 1) as it:
            run(it * 2, 0, True, True, True, True)
            run(it * 2 + 1, 1, True, True, True, True)
        with e.Fori(0, B - 1) as b:
            last = b * H + (H - 2)
            run(last, 0, True, True, True, True, b + 1)
            run(last + 1, 1, True, True, True, True, b + 1)
            with e.Fori(1, H // 2) as it:
                first = b * H + it * 2 + (H - 2)
                run(first, 0, True, True, True, True)
                run(first + 1, 1, True, True, True, True)
        run(HEADS - 2, 0, True, True, True, True)
        run(HEADS - 1, 1, True, True, False, True)
        run(HEADS, 0, False, True, False, True)

    flat_v = [v[:, :, :, :].rearrange("p a t d -> p (a t d)") for v in V]
    ffn_w = [xT[:, a, :, :].rearrange("p t n -> p (t n)") for a in range(2)] + [flat_v[0]]
    x1T = [t.rearrange("p (a t q) -> p a t q", a=2, t=KT)
           for t in (flat_v[1], OT[0][:, :, :].rearrange("p a n -> p (a n)"))]
    fuse = [q[:, :, :, :].rearrange("p a b n -> p (a b n)").rearrange("p (a j q) -> p a j q", a=2, q=GQ)
            for q in QK]
    fuse_f, silu = proj, swap
    down_s = norm_o[:, :, :].rearrange("p b (t c) -> p b t c", c=DIM)
    down_psum = [x[:, :].rearrange("p (t c) -> p t c", c=DIM) for x in (O, PJ)]
    x1 = rot[:, :, 0:DIM]
    w8_in, w_ready, half_in, x1_in = (sem(n) for n in ("w8_in", "w_ready", "half_in", "x1_in"))
    summed, measured, averaged, eps_in, powed = (
        [sem(f"{n}{w}") for w in (1, 2)] for n in ("summed", "measured", "averaged", "eps_in", "powed"))
    x1_done, y_done, out_done = (sem(n) for n in ("x1_done", "y_done", "out_done"))
    normalised = (x1_done, y_done)
    xt_up, xt_hi, xt_lo, gate_up, silued, fused, fuse_hi, fuse_lo, downed, down_read = (
        sem(n) for n in ("xt_up", "xt_hi", "xt_lo", "gate_up", "silued", "fused", "fuse_hi", "fuse_lo", "downed",
                         "down_read"))
    DOWN_AFTER = {0: [-2], 1: [-1], 2: [], 3: [0, 1], 4: [2], 5: [3], 6: [4], 7: [5]}

    def groups(e, run):
        run(0, 0, True, True)
        with e.Fori(0, (FG - 2) // 2) as it:
            run(it * 2 + 1, 1, False, True)
            run(it * 2 + 2, 0, False, True)
        run(FG - 1, 1, False, False)

    with nc.Block() as block:

        @block.sync
        def _(sp):
            for half, loaded in ((0, x_first), (1, x_in)):
                sp.dma_start(halves(x_raw, None, half), x_cols[0][:, :, half * GQ:(half + 1) * GQ].rearrange(
                    "t p n -> p t n")).then_inc(loaded, 16)
            for dst, src in ((bqk[:, :, :], bias_qk), (cos_t[:, :], rope_cos), (sin_t[:, :], rope_sin),
                             (ident[:, :], ident_in), (rot[:, 0, 0:P], mask_in), (bv_t[:, :], bias_v),
                             (sg_t[:, 0, :], s_gate), (sg_t[:, 1, :], s_up),
                             (bo_b[:, :], bias_o.to_broadcast([P, DIM])),
                             (sd_b[:, :], s_down.to_broadcast([P, DIM]))):
                sp.dma_start(dst, src).then_inc(consts_in, 16)
            def run(n, par, own, prev, project, out_proj, next_x=None):
                for s in range(8):
                    if project and s < 4:
                        m, c = n + 1, s
                        sp.wait_ge(chunk_sb, n_four(m, c))
                        for lo, hi in ((0, D // 2), (D // 2, 0)):
                            sp.dma_start(swap[lo:lo + D // 2, c % 2, :],
                                         proj[hi:hi + D // 2, c % 2, :]).then_inc(swapped[c % 2], 16)
                    if isinstance(n, int) and n == 0 and s == 6:
                        for b in range(B):
                            sp.dma_start(resid[:, b * NT:(b + 1) * NT, :], x_rows[b]).then_inc(resid_in, 16)
                    if isinstance(n, int) and n == HEADS - 2 and s == 0:
                        sp.wait_ge(x_lo, n_x(B - 1, 1))
                        for i, src in enumerate((wg8, wu8, wd8)):
                            sp.dma_start(w32[:, i, :], src).then_inc(w8_in, 16)
                    if prev and s in (1, 2):
                        reciprocals(n - 1, 1, s == 1)
                    if own and s in (4, 5):
                        reciprocals(n, 0, s == 4)
                    if s == 0 and par == 0 and next_x is not None:
                        sp.wait_ge(x_lo, n_x(next_x - 1, 1))
                        sp.dma_start(x_raw[:, :, :], x_cols[bass.ds(next_x, 1)].rearrange("b t p n -> p (b t) n")
                                     ).then_inc(x_in, 16)

            def reciprocals(n, g, out_part):
                if out_part:
                    sp.wait_ge(recip_ok, n_group(n, g))
                    sp.dma_start(recip_d[g].rearrange("(p t) -> p t", p=P), recip[:, g, :]
                                 ).then_inc(recip_out, 16)
                else:
                    sp.wait_ge(recip_out, 16 * n_group(n, g))
                    sp.dma_start(recip_b[:, g, :], recip_d[g:g + 1, :].to_broadcast([P, GQ])
                                 ).then_inc(recip_in[g], 16)

            sequence_timelines(sp, run)

            out_v = out.rearrange("(g t p) c -> g p t c", t=TPG, p=P)
            with sp.Fori(0, FG) as g:
                sp.wait_ge(y_done, 4 * g + 4)
                sp.dma_start(out_v[bass.ds(g, 1)].rearrange("g p t c -> (g p) t c"),
                             resid[:, bass.ds(g * TPG, TPG), :]).then_inc(out_done, 16)
            sp.wait_ge(out_done, 16 * FG)

        @block.gpsimd
        def _(pool):
            def run(n, par, own, prev, project, out_proj, next_x=None):
                m = n + 1
                for s in range(8):
                    if isinstance(n, int) and n == HEADS - 1 and s == 2:
                        inverse_root(0, 0)
                    if prev and par == 0 and s == 0:
                        pool.wait_ge(WO_hi, n >> 1)
                        nc.gpsimd.tensor_tensor(WO[:, :, 1, :], wo_raw[:, :, :], WO[:, :, 0, :].bitcast(F32),
                                                ALU.subtract).then_inc(WO_lo, 1)
                    if prev and s in (1, 7):
                        g = s // 4
                        q, o = (1 - par) , slice(g * GQ, (g + 1) * GQ)
                        pool.wait_ge(o_hi, n_group(n - 1, g))
                        nc.gpsimd.tensor_tensor(norm_o[:, g, :], norm_o[:, g, :],
                                                bias_o_m[:, q:q + 1].to_broadcast([P, GQ]),
                                                ALU.add).then_inc(o_biased, 1)
                        pool.wait_ge(o_biased, n_group(n - 1, g))
                        nc.gpsimd.tensor_tensor(OT[q][:, 1, o], norm_o[:, g, :], OT[q][:, 0, o].bitcast(F32),
                                                ALU.subtract).then_inc(o_lo, 1)
                    if project and 1 <= s < 5:
                        c = s - 1
                        pool.wait_ge(swapped[c % 2], 32 * (2 * m + (c // 2 + 1)))
                        half = slice((c // 2) * GQ, (c // 2 + 1) * GQ)
                        nc.gpsimd.tensor_tensor(swap[:, c % 2, :], swap[:, c % 2, :], sin_t[:, half],
                                                ALU.mult).then_inc(sin_done, 1)
                    if next_x is not None and (par, s) in ((0, 6), (1, 0)):
                        pool.wait_ge(x_hi, n_x(next_x, par))
                        nc.gpsimd.tensor_tensor(halves(xT, 1, par), halves(x_raw, None, par),
                                                halves(xT, 0, par).bitcast(F32), ALU.subtract).then_inc(x_lo, 1)
                    if project and 3 <= s < 7:
                        c = s - 3
                        pool.wait_ge(rot_hi, n_four(m, c))
                        half = slice((c // 2) * GQ, (c // 2 + 1) * GQ)
                        q = QK[1 - par]
                        nc.gpsimd.tensor_tensor(q[:, c % 2, 1, half], rot[:, c, :],
                                                q[:, c % 2, 0, half].bitcast(F32),
                                                ALU.subtract).then_inc(rot_lo, 1)
                    if n_has(n, project) and w_piece(n, s) in range(3):
                        w_low(n + 2, par, w_piece(n, s))

            def w_low(m, buf, q):
                pool.wait_ge(w_hi, n_w(m, q))
                nc.gpsimd.tensor_tensor(W[buf][:, q, 1, :, :], w_raw[:, q, :, :],
                                        W[buf][:, q, 0, :, :].bitcast(F32), ALU.subtract).then_inc(w_lo, 1)

            pool.wait_ge(consts_in, 16 * 10)
            pool.wait_ge(w_lo, 3)
            pool.wait_ge(x_lo, 2)
            nc.gpsimd.memset(minus_half[:, :], -0.5).then_inc(half_in, 1)
            pool.wait_ge(half_in, 1)

            def inverse_root(w, g):
                pool.wait_ge(eps_in[w], g + 1)
                wait(pool, normalised[w], TPG * g)
                nc.gpsimd.tensor_tensor(rstd[:, w, :], var_eps[:, w, :], minus_half[:, :], ALU.pow
                                        ).then_inc(powed[w], 1)

            sequence_timelines(pool, run)

            def group(g, par, first, more):
                for j in range(JT):
                    pool.wait_ge(fuse_hi, 8 * g + (j + 1))
                    nc.gpsimd.tensor_tensor(fuse[j % 2][:, 1, j // 2, :], fuse_f[:, j % 2, :],
                                            fuse[j % 2][:, 0, j // 2, :].bitcast(F32),
                                            ALU.subtract).then_inc(fuse_lo, 1)
                    if more and j == 1:
                        inverse_root(0, g + 1)
                    if not first and j == 4:
                        inverse_root(1, g - 1)

            groups(pool, group)
            inverse_root(1, FG - 1)

        @block.scalar
        def _(act):
            copy = lambda o, i: nc.scalar.activation(o, i, ACT.Copy)
            act.dma_start(w_raw[:, :, :, :], w_heads[0].rearrange("p (q t c) -> p q t c", q=3, t=KT)
                          ).then_inc(W_in, 16)

            def x_high(b, half):
                if isinstance(b, int) and half == 0:
                    act.wait_ge(x_first, 16)
                else:
                    act.wait_ge(x_in, b * 16 + 16)
                copy(halves(xT, 0, half), halves(x_raw, None, half)).then_inc(x_hi, 1)

            def w_high(m, buf, q):
                act.wait_ge(W_in, 16 * (m + 1))
                copy(W[buf][:, q, 0, :, :].rearrange("p t c -> p (t c)"),
                     w_raw[:, q, :, :].rearrange("p t c -> p (t c)")).then_inc(w_hi, 1)

            def head_column(m):
                return slice(m % H, m % H + 1) if isinstance(m, int) else bass.ds(m & (H - 1), 1)

            def projection_bias(m, buf):
                nc.scalar.copy(bias_m[:, buf, :], bqk[:, :, head_column(m)].rearrange("p b h -> p (b h)")
                               ).then_inc(bias_at, 1)

            def load_w(m):
                act.wait_ge(w_lo, n_w(m - 1, 2))
                src = w_heads[m % H] if isinstance(m, int) else \
                    w_heads[bass.ds(m & (H - 1), 1), :, :].rearrange("b p n -> (b p) n")
                act.dma_start(w_raw[:, :, :, :], src.rearrange("p (q t c) -> p q t c", q=3, t=KT)
                              ).then_inc(W_in, 16)

            w_high(0, 0, 0)
            x_high(0, 0)
            for q in (1, 2):
                w_high(0, 0, q)
            x_high(0, 1)
            load_w(1)
            act.wait_ge(consts_ready, 2)
            projection_bias(0, 0)

            def run(n, par, own, prev, project, out_proj, next_x=None):
                m, nxt = n + 1, 1 - par
                for s in range(8):
                    if s < 4:
                        if own:
                            softmax(n, s)
                        if project:
                            chunk_out(m, nxt, s)
                        if isinstance(n, int) and n == HEADS - 1:
                            ffn_weights(s)
                        if prev:
                            probs_hi(n, 2 * s)
                            probs_hi(n, 2 * s + 1)
                    if next_x is not None and (par, s) in ((0, 6), (1, 0)):
                        act.wait_ge(v_made, n_four(m, 1) if par == 0 else n_four(n, 3))
                        x_high(next_x, par)
                    if s >= 4 and project:
                        v = s - 4
                        act.wait_ge(v_made, n_four(m, v))
                        wait(act, attended, n_step(n, 7))
                        copy(V[nxt][:, 0, 2 * v:2 * v + 2, :],
                             v_psum[:, :, 0, :]).then_inc(v_hi, 1)
                    if s >= 4 and own:
                        probs_hi(n, s + 4)
                    if own and s >= 4:
                        softmax(n, s)
                    if isinstance(n, int) and n == HEADS and s == 4:
                        for t in range(TPG):
                            fixed_x1(0, t)
                    if prev and s in (0, 4):
                        g = s // 4
                        o = slice(g * GQ, (g + 1) * GQ)
                        act.wait_ge(o_norm, n_group(n - 1, g))
                        act.wait_ge(bias_o_at, n)
                        if not isinstance(n, int) or n > 2:
                            act.wait_ge(added, n_added(n, -1) if par == 0 else n_added(n - 1, 2 * g + 1))
                        nc.scalar.activation(OT[nxt][:, 0, o], norm_o[:, g, :], ACT.Identity,
                                             bias=bias_o_m[:, nxt:nxt + 1]).then_inc(o_hi, 1)
                    if isinstance(n, int) and n == HEADS and s == 5:
                        for t in range(KT):
                            x1T_high(0, 0, t)
                    if project and 3 <= s < 7:
                        c = s - 3
                        half = slice((c // 2) * GQ, (c // 2 + 1) * GQ)
                        act.wait_ge(rot_done, n_four(m, c))
                        copy(QK[nxt][:, c % 2, 0, half], rot[:, c, :]).then_inc(rot_hi, 1)
                    if n_has(n, project) and w_piece(n, s) in range(3):
                        w_high(n + 2, par, w_piece(n, s))
                    if s == 5 and n_has(n, project):
                        projection_bias(n + 2, par)
                    if s == 5 and own:
                        wait(act, o_lo, n_group(n - 2, 1))
                        nc.scalar.copy(bias_o_m[:, par:par + 1], bv_t[:, head_column(n)]).then_inc(bias_o_at, 1)
                    if w_piece(n, s) == 3 and project and not (isinstance(n, int) and n + 3 >= HEADS):
                        load_w(n + 3)
                    if s == 3 and par == 1 and own:
                        wait(act, WO_lo, (n - 1) >> 1)
                        pair = (n - 1) >> 1
                        src = wo_heads[pair % (H // 2)] if isinstance(n, int) else \
                            wo_heads[bass.ds(pair & (H // 2 - 1), 1), :, :].rearrange("b p n -> (b p) n")
                        act.dma_start(wo_raw[:, :, :], src.rearrange("p (h c) -> p h c", h=2)).then_inc(WO_in, 16)
                    if s == 7 and par == 1 and own:
                        wait(act, wo_made, 2 * (n - 1))
                        act.wait_ge(WO_in, 8 * (n + 1))
                        copy(WO[:, :, 0, :], wo_raw[:, :, :]).then_inc(WO_hi, 1)

            def probs_hi(n, k):
                g, j, c0 = step(k)
                act.wait_ge(transposed, n_step(n, k))
                wait(act, attended, n_step(n, k) - 2)
                copy(PT[:, k % 2, 0, c0:], TP[k % 2][:, c0:]).then_inc(pt_hi, 1)

            def softmax(n, s):
                g, i, cols = s // TPG, s % TPG, (s + 1) * P
                act.wait_ge(maxed, n_scored(n, s))
                wait(act, transposed, n_step(n, 7) if g else n_step(n - 1, 11))
                wait(act, recip_ok, n_group(n - 1, g))
                nc.scalar.activation(prob[g][:, prob_at[g][i]:prob_at[g][i] + cols], S[s % 2][:, 0:cols], ACT.Exp,
                                     bias=neg_max[:, s:s + 1], scale=1.0,
                                     accum_out=row_sum[:, s:s + 1]).then_inc(exped, 1)

            def chunk_out(m, m_par, c):
                act.wait_ge(chunked, n_four(m, c))
                act.wait_ge(bias_at, m + 1)
                wait(act, rot_done, n_four(m, c) - 2)
                nc.scalar.activation(proj[:, c % 2, :], S[c % 2][:, GQ:], ACT.Identity,
                                     bias=bias_m[:, m_par, c % 2:c % 2 + 1],
                                     scale=SCALE if c % 2 == 0 else 1.0).then_inc(chunk_sb, 1)

            def ffn_weights(piece):
                i, cols = piece // 2, slice((piece % 2) * INTER, (piece % 2 + 1) * INTER)
                act.wait_ge(w8_in, 48)
                act.wait_ge(v_made, n_four(HEADS - 1, 3))
                copy(ffn_w[i][:, cols], w8[:, i, cols]).then_inc(w_ready, 1)

            def fixed_x1(g, t):
                at = g * TPG + t
                row = resid[:, at, :] if isinstance(at, int) else \
                    resid[:, bass.ds(at, 1), :].rearrange("p a c -> p (a c)")
                act.wait_ge(x1_done, TPG * g + (t + 1))
                wait(act, xt_up, 2 * g)
                copy(x1[:, t, :], row).then_inc(x1_in, 1)

            def x1T_high(g, par, t):
                act.wait_ge(xt_up, KT * g + (t + 1))
                copy(x1T[par][:, 0, t, :], TP[t][:, :]).then_inc(xt_hi, 1)

            sequence_timelines(act, run)

            def group(g, par, first, more):
                for j in range(JT):
                    act.wait_ge(gate_up, 16 * g + (2 * j + 1))
                    wait(act, fused, 8 * g + (j - 1))
                    nc.scalar.activation(silu[:, j % 2, :], S[j % 2][:, 0:GQ], ACT.Silu,
                                         scale=sg_t[:, 0, j:j + 1]).then_inc(silued, 1)
                    act.wait_ge(fused, 8 * g + (j + 1))
                    wait(act, downed, 8 * (g - 1) + (j + 1))
                    copy(fuse[j % 2][:, 0, j // 2, :], fuse_f[:, j % 2, :]).then_inc(fuse_hi, 1)
                    if more and j == 4:
                        for t in range(TPG):
                            fixed_x1(g + 1, t)
                    if more and j == 6:
                        for t in range(KT):
                            x1T_high(g + 1, 1 - par, t)

            groups(act, group)

        @block.vector
        def _(dve):
            sub = lambda o, a, b: nc.vector.tensor_tensor(o, a, b, ALU.subtract)
            dve.wait_ge(w_hi, 1)
            sub(W[0][:, 0, 1, :, :], w_raw[:, 0, :, :], W[0][:, 0, 0, :, :].bitcast(F32)).then_inc(w_lo, 1)
            for half in range(2):
                dve.wait_ge(x_hi, half + 1)
                sub(halves(xT, 1, half), halves(x_raw, None, half), halves(xT, 0, half).bitcast(F32)
                    ).then_inc(x_lo, 1)
                for q in ((1, 2) if half == 0 else ()):
                    dve.wait_ge(w_hi, q + 1)
                    sub(W[0][:, q, 1, :, :], w_raw[:, q, :, :], W[0][:, q, 0, :, :].bitcast(F32)).then_inc(w_lo, 1)
            dve.wait_ge(consts_in, 16 * 10)
            nc.vector.tensor_copy(ident_b[:, :], ident[:, :]).then_inc(consts_ready, 1)
            nc.vector.tensor_scalar(bqk[:, 0, :], bqk[:, 0, :], SCALE, None, ALU.mult).then_inc(consts_ready, 1)
            nc.vector.tensor_copy(mask_b[:, :], rot[:, 0, 0:P]).then_inc(consts_ready, 1)
            nc.vector.memset(zeros[:, :], 0.0).then_inc(consts_ready, 1)
            dve.wait_ge(consts_ready, 4)

            def run(n, par, own, prev, project, out_proj):
                m, nxt = n + 1, 1 - par
                for s in range(8):
                    if isinstance(n, int) and n == 1 and s == 7:
                        dve.wait_ge(resid_in, 16 * B)
                        nc.vector.memset(stats[:, 0, 0, :], 0.0).then_inc(added, 4)
                    if isinstance(n, int) and n == HEADS - 1:
                        if s == 0:
                            dve.wait_ge(added, n_added(HEADS - 2, 1))
                            first_sums(0)
                        if s == 1:
                            moments(0, 0)
                        if s == 3:
                            normalise(0, 0)
                        if s == 5:
                            ffn_down_weights()
                    if isinstance(n, int) and n == HEADS and s == 5:
                        x1T_low(0, 0)
                    if own:
                        dve.wait_ge(scored, n_scored(n, s))
                        nc.vector.tensor_reduce(neg_max[:, s:s + 1], S[s % 2][:, 0:(s + 1) * P], AX.X, ALU.max,
                                                negate=True).then_inc(maxed, 1)
                    if prev and s in (0, 4):
                        g = s // 4
                        dve.wait_ge(attended, n_step(n - 1, 11) if g == 0 else n_step(n, 7))
                        dve.wait_ge(recip_in[g], 16 * n)
                        wait(dve, o_lo, n_group(n - 1, g) - 2)
                        by_tile = lambda x: x.rearrange("d (t p) -> d t p", p=P)
                        nc.vector.tensor_tensor(by_tile(norm_o[:, g, :]), by_tile(O[:, :]),
                                                recip_b[:, g, :].rearrange("d (p t) -> d t p", p=P),
                                                ALU.mult).then_inc(o_norm, 1)
                    if s >= 4 and project:
                        v = s - 4
                        dve.wait_ge(v_hi, n_four(m, v))
                        wait(dve, v_lo, n_four(m, v) - 1)
                        tiles = slice(2 * v, 2 * v + 2)
                        sub(v_rest[:, :, :], v_psum[:, :, 0, :], V[nxt][:, 0, tiles, :].bitcast(F32)
                            ).then_inc(v_sub, 1)
                        dve.wait_ge(v_sub, n_four(m, v))
                        nc.vector.tensor_tensor(V[nxt][:, 1, tiles, :], v_rest[:, :, :], v_psum[:, :, 1, :],
                                                ALU.add).then_inc(v_lo, 1)
                    if s >= 4 and own:
                        probs_lo(n, s + 4)
                    if project and 2 <= s < 6:
                        c = s - 2
                        dve.wait_ge(sin_done, n_four(m, c))
                        dve.wait_ge(cos_done, n_four(m, c))
                        nc.vector.tensor_tensor(rot[:, c, :], rot[:, c, :], swap[:, c % 2, :],
                                                ALU.add).then_inc(rot_done, 1)
                    done = output_of(n, par, s, out_proj)
                    if done:
                        add_output(s, *done)
                    if s < 4 and prev:
                        probs_lo(n, 2 * s)
                    if s < 3 and project:
                        rotate_cos(s, m)
                    if s < 4 and prev:
                        probs_lo(n, 2 * s + 1)
                    if s == 3 and project:
                        rotate_cos(s, m)
                    if own and s == 4:
                        reciprocal(n, 0)
                    if prev and s == 0:
                        reciprocal(n - 1, 1)

            def probs_lo(n, k):
                g, j, c0 = step(k)
                dve.wait_ge(pt_hi, n_step(n, k))
                sub(PT[:, k % 2, 1, c0:], TP[k % 2][:, c0:],
                    PT[:, k % 2, 0, c0:].bitcast(F32)).then_inc(pt_lo, 1)

            def add_output(s, n, i):
                dve.wait_ge(wo_made, n_made(n, i))
                dve.wait_ge(added, n_added(n, -1))
                if isinstance(n, int):
                    at = ((n - 2) // H) * NT + 2 * i
                    rows = resid[:, at:at + 2, :]
                else:
                    rows = resid[:, bass.ds((((n - 2) >> 4) & (B - 1)) * NT + 2 * i, 2), :]
                rows = rows.rearrange("p a c -> p (a c)")
                nc.vector.tensor_tensor(rows, rows, output_bank(s), ALU.add).then_inc(added, 1)

            def rotate_cos(c, m):
                half = slice((c // 2) * GQ, (c // 2 + 1) * GQ)
                dve.wait_ge(chunk_sb, n_four(m, c))
                wait(dve, rot_lo, n_four(m - 1, c))
                nc.vector.tensor_tensor(rot[:, c, :], proj[:, c % 2, :], cos_t[:, half],
                                        ALU.mult).then_inc(cos_done, 1)

            def reciprocal(n, g):
                dve.wait_ge(exped, n_scored(n, 4 * g + 3))
                wait(dve, recip_out, 16 * (n_group(n, g) - 2))
                nc.vector.reciprocal(recip[:, g, :], row_sum[:, 4 * g:4 * g + 4]).then_inc(recip_ok, 1)

            def ffn_down_weights():
                dve.wait_ge(w8_in, 48)
                dve.wait_ge(attended, n_step(HEADS - 1, 7))
                nc.vector.tensor_copy(ffn_w[2], w8[:, 2, :]).then_inc(w_ready, 1)

            def rows(g, t, count=1):
                at = g * TPG + t
                return (resid[:, at:at + count, :] if isinstance(at, int) else resid[:, bass.ds(at, count), :]
                        ).rearrange("p a c -> p (a c)")

            def by_two(x):
                return x.unsqueeze(1).to_broadcast([P, 2, DIM])

            def moments(w, g):
                for t in range(TPG):
                    dve.wait_ge(summed[w], 2 * g + (t // 2 + 1))
                    wait(dve, averaged[w], TPG * g)
                    dve.nop(nofuse=True)
                    nc.vector.bn_stats(stats[:, w, t, :], rows(g, t)).then_inc(measured[w], 1)
                for t in range(TPG):
                    dve.wait_ge(measured[w], TPG * g + (t + 1))
                    wait(dve, normalised[w], TPG * g)
                    dve.nop(nofuse=True)
                    nc.vector.bn_aggr(mv[:, w, t, :], stats[:, w, t, :]).then_inc(averaged[w], 1)
                dve.wait_ge(averaged[w], TPG * g + TPG)
                wait(dve, powed[w], g)
                nc.vector.tensor_scalar(var_eps[:, w, :], mv[:, w, :, 1], EPS, None, ALU.add).then_inc(eps_in[w], 1)

            def normalise(w, g):
                dve.wait_ge(powed[w], g + 1)
                for t in range(TPG):
                    nc.vector.tensor_scalar(rows(g, t), rows(g, t), mv[:, w, t, 0:1], rstd[:, w, t:t + 1],
                                            ALU.subtract, ALU.mult).then_inc(normalised[w], 1)

            def first_sums(g):
                for pair in range(2):
                    two = rows(g, 2 * pair, 2)
                    nc.vector.tensor_tensor(two.rearrange("p (a c) -> p a c", a=2), two.rearrange(
                        "p (a c) -> p a c", a=2), by_two(bo_b[:, :]), ALU.add).then_inc(summed[0], 1)

            def down_scaled(g):
                for pair in range(2):
                    dve.wait_ge(downed, 8 * g + JT)
                    dve.wait_ge(summed[1], 2 * g)
                    nc.vector.tensor_tensor(down_s[:, pair, :, :], down_psum[pair], by_two(sd_b[:, :]),
                                            ALU.mult).then_inc(down_read, 1)

            def second_sums(g):
                for pair in range(2):
                    two = rows(g, 2 * pair, 2)
                    dve.wait_ge(down_read, 2 * g + (pair + 1))
                    dve.wait_ge(x1_done, TPG * g + TPG)
                    nc.vector.tensor_tensor(two, two, down_s[:, pair, :, :].rearrange("p t c -> p (t c)"),
                                            ALU.add).then_inc(summed[1], 1)

            def x1T_low(g, par):
                for t in range(KT):
                    dve.wait_ge(xt_hi, KT * g + (t + 1))
                    sub(x1T[par][:, 1, t, :], TP[t][:, :], x1T[par][:, 0, t, :].bitcast(F32)).then_inc(xt_lo, 1)

            timelines(dve, run)

            def group(g, par, first, more):
                for j in range(JT):
                    if j == 2 and not first:
                        down_scaled(g - 1)
                    dve.wait_ge(gate_up, 16 * g + (2 * j + 2))
                    dve.wait_ge(silued, 8 * g + (j + 1))
                    wait(dve, fuse_lo, 8 * g + (j - 1))
                    nc.vector.scalar_tensor_tensor(fuse_f[:, j % 2, :], S[j % 2][:, GQ:], sg_t[:, 1, j:j + 1],
                                                   silu[:, j % 2, :], ALU.mult, ALU.mult).then_inc(fused, 1)
                    if more and j == 0:
                        first_sums(g + 1)
                    if more and j == 1:
                        moments(0, g + 1)
                    if not first and j == 2:
                        second_sums(g - 1)
                    if more and j == 3:
                        normalise(0, g + 1)
                    if not first and j == 4:
                        moments(1, g - 1)
                    if not first and j == 6:
                        normalise(1, g - 1)
                    if more and j == 6:
                        x1T_low(g + 1, 1 - par)

            groups(dve, group)
            down_scaled(FG - 1)
            second_sums(FG - 1)
            moments(1, FG - 1)
            normalise(1, FG - 1)

        @block.tensor
        def _(pe):
            mm = nc.tensor.matmul
            def run(n, par, own, prev, project, out_proj):
                m, nxt = n + 1, 1 - par

                def scores(s):
                    q, k = QK[par][:, 0], QK[par][:, 1]
                    pe.wait_ge(rot_lo, n_four(n, 1 if s < 4 else 3))
                    wait(pe, exped, n_scored(n, s) - 2)
                    if isinstance(n, int) and n == 0 and s == 0:
                        pe.wait_ge(consts_ready, 4)
                    if s >= 4:
                        wait(pe, chunk_sb, n_four(m, s % 2 + 2) if project else 0)
                    output_read(s)
                    cols = (s + 1) * P
                    banks = [(a, min(a + GQ, cols)) for a in range(0, cols, GQ)]
                    for part_q, part_k in ((0, 0), (0, 1), (1, 0)):
                        for a, b in banks:
                            mm(S[s % 2][:, a:b], QK[par][:, 0, part_q, s * P:(s + 1) * P],
                               QK[par][:, 1, part_k, a:b], start=(part_q, part_k) == (0, 0),
                               stop=part_q == 1 and b != cols)
                    mm(S[s % 2][:, cols - P:cols], ident_b[:, :], mask_b[:, :], start=False, stop=True
                       ).then_inc(scored, 1)

                def transposes(k):
                    g, j, c0 = step(k)
                    pe.wait_ge(exped, n_scored(n, 3) if g == 0 else n_scored(n - 1, 7))
                    wait(pe, pt_lo, n_step(n, k) - 2)
                    for i in range(c0 // P, TPG):
                        last = nc.tensor.transpose(TP[k % 2][:, i * P:(i + 1) * P],
                                                   prob[g][:, prob_at[g][i] + j * P:prob_at[g][i] + (j + 1) * P],
                                                   ident[:, :])
                    last.then_inc(transposed, 1)

                def attend(nn, k, who):
                    g, j, c0 = step(k)
                    if j == 0:
                        head = nn - 1 if g else nn
                        pe.wait_ge(v_lo, n_four(head, 3))
                        wait(pe, o_norm, n_group(head, g) - 1)
                    pe.wait_ge(pt_lo, n_step(nn, k))
                    v = V[who]
                    last_j = TPG * (g + 1) - 1
                    mm(O[:, c0:], v[:, 0, j, :], PT[:, k % 2, 0, c0:], start=j == 0, stop=False)
                    mm(O[:, c0:], v[:, 1, j, :], PT[:, k % 2, 0, c0:], start=False, stop=False)
                    mm(O[:, c0:], v[:, 0, j, :], PT[:, k % 2, 1, c0:], start=False, stop=j == last_j
                       ).then_inc(attended, 1)

                def chunk(c):
                    half = slice((c // 2) * GQ, (c // 2 + 1) * GQ)
                    if c < 2:
                        pe.wait_ge(w_lo, n_w(m, c))
                    if c % 2 == 0:
                        pe.wait_ge(x_lo, n_x(m >> 4, c // 2))
                    wait(pe, exped, n_scored(n, c) - 2 if own else n_scored(n - 1, 7))
                    if c >= 2:
                        pe.wait_ge(chunk_sb, n_four(m, c) - 2)
                    output_read(c)
                    for i, (pw, px) in enumerate(((0, 0), (0, 1), (1, 0))):
                        for t in range(KT):
                            last = mm(S[c % 2][:, GQ:], W[nxt][:, c % 2, pw, t, :], xT[:, px, t, half],
                                      start=i == 0 and t == 0, stop=i == 2 and t == KT - 1)
                    last.then_inc(chunked, 1)

                def v_pair(v):
                    wait(pe, v_lo, n_four(m, v) - 1)
                    if v == 0:
                        pe.wait_ge(w_lo, n_w(m, 2))
                    for t2 in range(2):
                        tok = slice((2 * v + t2) * P, (2 * v + t2 + 1) * P)
                        w = W[nxt][:, 2]
                        mm(v_psum[:, t2, :, :], xT[:, 0, 0, tok], w[:, :, 0, :], start=True, stop=False)
                        for t in range(KT):
                            mm(v_psum[:, t2, 0, :], xT[:, 1, t, tok], w[:, 0, t, :], start=False, stop=False)
                        last = mm(v_psum[:, t2, :, :], xT[:, 0, 1, tok], w[:, :, 1, :],
                                  start=False, stop=True)
                    last.then_inc(v_made, 1)

                def output_read(s):
                    before = output_of(n, par, s - 1, out_proj)
                    if before:
                        pe.wait_ge(added, n_added(*before))

                def output(s, nn, i):
                    if i == 0:
                        pe.wait_ge(WO_lo, nn >> 1)
                    pe.wait_ge(o_lo, n_group(nn - 1, i // 2))
                    if project:
                        pe.wait_ge(chunk_sb, n_four(m, s - 1))
                    pe.wait_ge(added, n_added(nn, i - 1))
                    for tile in range(2):
                        tok = slice((2 * i + tile) * P, (2 * i + tile + 1) * P)
                        order = [(h, a, b) for h in range(2) for a, b in ((0, 0), (0, 1), (1, 0))]
                        for z, (h, po, pw) in enumerate(order):
                            last = mm(output_bank(s)[:, tile * DIM:(tile + 1) * DIM], OT[h][:, po, tok],
                                      WO[:, h, pw, :], start=z == 0, stop=z == len(order) - 1)
                    last.then_inc(wo_made, 1)

                for s in range(8):
                    if own:
                        scores(s)
                    if s < 4 and project:
                        chunk(s)
                    made = output_of(n, par, s, out_proj)
                    if made:
                        output(s, *made)
                    if prev and s == 0:
                        attend(n - 1, 11, nxt)
                        transposes(0)
                        transposes(1)
                    elif prev and s < 4:
                        attend(n, 2 * s - 2, nxt)
                        transposes(2 * s)
                        attend(n, 2 * s - 1, nxt)
                        transposes(2 * s + 1)
                    if isinstance(n, int) and n == HEADS and s == 5:
                        x1_transposes(0)
                    if s == 4 and prev:
                        attend(n, 6, nxt)
                        attend(n, 7, nxt)
                    if s == 4 and project:
                        v_pair(0)
                    if s >= 4 and own:
                        transposes(s + 4)
                    if s > 4 and project:
                        v_pair(s - 4)
                    if s > 4 and own:
                        attend(n, s + 3, par)


            def x1_transposes(g):
                pe.wait_ge(x1_in, g * TPG + TPG)
                wait(pe, xt_lo, 2 * g)
                for t in range(KT):
                    for i in range(TPG):
                        last = nc.tensor.transpose(TP[t][:, i * P:(i + 1) * P], x1[:, i, t * P:(t + 1) * P],
                                                   ident[:, :])
                    last.then_inc(xt_up, 1)

            timelines(pe, run)
            pe.wait_ge(added, n_added(HEADS, 3))
            pe.wait_ge(w_ready, 5)

            def down(g, j):
                pe.wait_ge(fuse_lo, 8 * g + (j + 1))
                if j == 0:
                    wait(pe, down_read, 2 * g)
                    for bank in (O, PJ):
                        mm(bank[:, :], zeros[:, 0:P], zeros[:, :], start=True, stop=False)
                for i in range(TPG):
                    for part in range(2):
                        last = mm(down_psum[i // 2][:, i % 2, :], fuse[j % 2][:, part, j // 2, i * P:(i + 1) * P],
                                  ffn_w[2].rearrange("p (j c) -> p j c", j=JT)[:, j, :],
                                  start=False, stop=j == JT - 1 and part == 1 and i % 2 == 1)
                last.then_inc(downed, 1)

            def group(g, par, first, more):
                pe.wait_ge(xt_lo, KT * g + KT)
                for j in range(JT):
                    wait(pe, silued, 8 * g + (j - 1))
                    wait(pe, fused, 8 * g + (j - 1))
                    for u in range(2):
                        for t in range(KT):
                            for part in range(2):
                                last = mm(S[j % 2][:, u * GQ:(u + 1) * GQ],
                                          ffn_w[u].rearrange("p (t c) -> p t c", t=KT)[:, t, j * P:(j + 1) * P],
                                          x1T[par][:, part, t, :], start=t == 0 and part == 0,
                                          stop=t == KT - 1 and part == 1)
                        last.then_inc(gate_up, 1)
                    for dj in DOWN_AFTER[j]:
                        if dj >= 0:
                            down(g, dj)
                        elif not first:
                            down(g - 1, dj + JT)
                    if more and j == 5:
                        x1_transposes(g + 1)

            groups(pe, group)
            for j in (JT - 2, JT - 1):
                down(FG - 1, j)


def rope_tables():
    inv = (1.0 / 10000.0 ** (np.arange(0, D, 2, dtype=np.float32) / np.float32(D))).astype(np.float32)
    f = (np.arange(N, dtype=np.float32)[:, None] * inv[None, :]).astype(np.float32)
    f = np.concatenate([f, f], axis=1).T.astype(np.float64)
    sign = np.where(np.arange(D) < D // 2, -1.0, 1.0)[:, None]
    return np.cos(f).astype(np.float32), (sign * np.sin(f)).astype(np.float32)


def kernel(**inputs):
    import concourse.bacc as _bacc
    from concourse.bass_utils import run_bass_kernel_spmd as _run

    a = {k.split("_", 1)[1]: np.asarray(v) for k, v in inputs.items()}
    x = a["attn_x"]
    cos, sin = rope_tables()

    def heads(w):
        return w.reshape(KT, P, H, P).transpose(2, 1, 0, 3)

    def words(w):
        return np.ascontiguousarray(w.transpose(1, 0, 2)).reshape(P, -1).view(np.int32)

    arrays = {
        "x_rows": x.reshape(B, NT, P, DIM).transpose(0, 2, 1, 3),
        "x_cols": x.transpose(0, 2, 1).reshape(B, KT, P, N),
        "w_heads": np.stack([heads(a["attn_Wq"]), heads(a["attn_Wk"]), heads(a["attn_Wv"])], axis=2
                            ).reshape(H, P, WQKV),
        "bias_qk": np.stack([a["attn_bq"].reshape(H, P).T, a["attn_bk"].reshape(H, P).T], axis=1),
        "bias_v": a["attn_bv"].reshape(H, P).T,
        "wo_heads": a["attn_Wo"].reshape(H // 2, 2, P, DIM).transpose(0, 2, 1, 3).reshape(H // 2, P, 2 * DIM),
        "bias_o": a["attn_bo"].reshape(1, DIM),
        "wg8": words(a["ffn_w_gate"].reshape(KT, P, INTER)),
        "wu8": words(a["ffn_w_up"].reshape(KT, P, INTER)),
        "wd8": words(a["ffn_w_down"].reshape(JT, P, DIM)),
        "s_gate": a["ffn_s_gate"].reshape(JT, P).T,
        "s_up": a["ffn_s_up"].reshape(JT, P).T,
        "s_down": a["ffn_s_down"].reshape(1, DIM),
        "rope_cos": cos,
        "rope_sin": sin,
        "ident_in": np.eye(P, dtype=np.float32),
        "mask_in": np.triu(np.full((P, P), MASKED, np.float32), k=1),
    }
    nc = _bacc.Bacc("TRN2", target_bir_lowering=False, num_devices=1)
    feed, args = {}, {}
    for name, v in arrays.items():
        v = np.ascontiguousarray(v)
        feed[f"in_{name}"] = v
        args[name] = nc.dram_tensor(f"in_{name}", v.shape, mybir.dt.from_np(v.dtype), kind="ExternalInput").ap()
    args["out"] = nc.dram_tensor("out", (B * N, DIM), F32, kind="ExternalOutput").ap()
    layer(nc, **args)
    r = _run(nc, [feed], core_ids=[0])
    return r.results[0]["out"].reshape(B, N, DIM)
```
